# Optimizing a Trainium2 kernel written in Bass

```python
import numpy as np
import jax
import jax.numpy as jnp

def _softmax(x, axis=-1):
    return jax.nn.softmax(x, axis=axis)
def _gelu(x):
    return jax.nn.gelu(x, approximate=True)
def _silu(x):
    return jax.nn.silu(x)
def _sigmoid(x):
    return jax.nn.sigmoid(x)
def _layernorm(x, axis=-1, eps=1e-5):
    m = jnp.mean(x, axis=axis, keepdims=True)
    v = jnp.var(x, axis=axis, keepdims=True)
    return (x - m) / jnp.sqrt(v + eps)
def _scatter_add(tgt, idx, src, axis=0):
    return tgt.at[idx].add(src)
def _segment_sum(src, seg, n):
    return jax.ops.segment_sum(src, seg, n)

kernel_name = 'mk_conv_preact_d1_conv_nhwc512_8095c8'

def setup_inputs(seed: int = 0):
    np.random.seed(seed)
    _w = jnp.asarray
    def _rec_inputs():
        import jax
        import jax.numpy as jnp
        _gk = jax.random.key(seed)
        x = -0.0005963 + 1.001 * jax.random.normal(jax.random.fold_in(_gk, 1), (2, 64, 48, 512), jnp.float32)
        return x
    x = _rec_inputs()
    def _L0_conv_setup():
        import jax, jax.numpy as jnp
        import numpy as np
        EMBED_DIM = 512
        N_HEADS = 8
        HEAD_DIM = EMBED_DIM // N_HEADS
        MAX_H = 64
        MAX_W = 48
        B, H, W = (2, 64, 48)

        def _rel_bias(rel_row_tab, rel_col_tab, height, width):
            row_idx = jnp.repeat(jnp.arange(height), width)
            col_idx = jnp.tile(jnp.arange(width), height)
            rel_row = jnp.clip(row_idx[:, None] - row_idx[None, :] + MAX_H - 1, 0, 2 * MAX_H - 2)
            rel_col = jnp.clip(col_idx[:, None] - col_idx[None, :] + MAX_W - 1, 0, 2 * MAX_W - 2)
            bias = rel_row_tab[rel_row] + rel_col_tab[rel_col]
            return jnp.transpose(bias, (2, 0, 1))
        key = jax.random.key(seed)
        k1, k2, k3, k4, k5 = jax.random.split(key, 5)
        x = jax.random.normal(k1, (B, H, W, EMBED_DIM), dtype=jnp.float32)
        w_qkv = jax.random.normal(k2, (EMBED_DIM, 3 * EMBED_DIM), dtype=jnp.float32) * EMBED_DIM ** (-0.5)
        w_out = jax.random.normal(k3, (EMBED_DIM, EMBED_DIM), dtype=jnp.float32) * EMBED_DIM ** (-0.5)
        rel_row_tab = jax.random.normal(k4, (2 * MAX_H - 1, N_HEADS), dtype=jnp.float32) * 0.02
        rel_col_tab = jax.random.normal(k5, (2 * MAX_W - 1, N_HEADS), dtype=jnp.float32) * 0.02
        return {'x': x, 'w_qkv': w_qkv, 'w_out': w_out, 'rel_row_tab': rel_row_tab, 'rel_col_tab': rel_col_tab}
    _L0_conv_all = _L0_conv_setup()
    _L0_conv_in = {k: v for k, v in _L0_conv_all.items() if k in ('w_qkv', 'w_out', 'rel_row_tab', 'rel_col_tab', )}
    del _L0_conv_all

    return {
        "x": x,
        "L0_conv_w_qkv": _L0_conv_in["w_qkv"],
        "L0_conv_w_out": _L0_conv_in["w_out"],
        "L0_conv_rel_row_tab": _L0_conv_in["rel_row_tab"],
        "L0_conv_rel_col_tab": _L0_conv_in["rel_col_tab"],
    }

def reference(x, L0_conv_w_qkv, L0_conv_w_out, L0_conv_rel_row_tab, L0_conv_rel_col_tab):
    import jax
    import jax.numpy as jnp
    def _L0_conv_ref(x, w_qkv, w_out, rel_row_tab, rel_col_tab):
        import jax, jax.numpy as jnp
        import numpy as np
        EMBED_DIM = 512
        N_HEADS = 8
        HEAD_DIM = EMBED_DIM // N_HEADS
        MAX_H = 64
        MAX_W = 48
        B, H, W = (2, 64, 48)

        def _rel_bias(rel_row_tab, rel_col_tab, height, width):
            row_idx = jnp.repeat(jnp.arange(height), width)
            col_idx = jnp.tile(jnp.arange(width), height)
            rel_row = jnp.clip(row_idx[:, None] - row_idx[None, :] + MAX_H - 1, 0, 2 * MAX_H - 2)
            rel_col = jnp.clip(col_idx[:, None] - col_idx[None, :] + MAX_W - 1, 0, 2 * MAX_W - 2)
            bias = rel_row_tab[rel_row] + rel_col_tab[rel_col]
            return jnp.transpose(bias, (2, 0, 1))
        b, h, w, d = x.shape
        s = h * w
        x_flat = x.reshape(b, s, d)
        qkv = x_flat @ w_qkv
        qkv = qkv.reshape(b, s, 3, N_HEADS, HEAD_DIM)
        qkv = jnp.transpose(qkv, (2, 0, 3, 1, 4))
        q, k, v = (qkv[0], qkv[1], qkv[2])
        scale = HEAD_DIM ** (-0.5)
        attn = jnp.einsum('bhqd,bhkd->bhqk', q, k) * scale
        attn = attn + _rel_bias(rel_row_tab, rel_col_tab, h, w)[None]
        attn = jax.nn.softmax(attn, axis=-1)
        out = jnp.einsum('bhqk,bhkd->bhqd', attn, v)
        out = jnp.transpose(out, (0, 2, 1, 3)).reshape(b, s, d)
        out = out @ w_out
        return out.reshape(b, h, w, d)

    def _gn(v, G=32, eps=1e-5):
        B_, H_, W_, C_ = v.shape
        g = v.reshape(B_, H_, W_, G, C_ // G)
        m = jnp.mean(g, axis=(1, 2, 4), keepdims=True)
        s = jnp.var(g, axis=(1, 2, 4), keepdims=True)
        return ((g - m) / jnp.sqrt(s + eps)).reshape(v.shape)

    def _ln_c(v, eps=1e-6):
        m = jnp.mean(v, axis=-1, keepdims=True)
        s = jnp.var(v, axis=-1, keepdims=True)
        return (v - m) / jnp.sqrt(s + eps)

    def _ln_t(v, eps=1e-5):
        m = jnp.mean(v, axis=-1, keepdims=True)
        s = jnp.var(v, axis=-1, keepdims=True)
        return (v - m) / jnp.sqrt(s + eps)

    def _to_tokens(v):
        B_, H_, W_, C_ = v.shape
        return v.reshape(B_, H_ * W_, C_)
    def _from_tokens(t, like):
        return t.reshape(like.shape)

    x = x + _L0_conv_ref(_gn(x), L0_conv_w_qkv, L0_conv_w_out, L0_conv_rel_row_tab, L0_conv_rel_col_tab)
    return x


_drawn_inputs = setup_inputs


def setup_inputs(seed=0):
    import zlib

    import numpy as np

    out = dict(_drawn_inputs(seed))
    spreads = {}
    factors = {'L0_conv_rel_row_tab': 64.0, 'L0_conv_rel_col_tab': 64.0}
    for name, (base, spread) in spreads.items():
        noise = np.random.default_rng([zlib.crc32(name.encode()), seed]).standard_normal(out[name].shape)
        drawn = base * np.exp(spread * noise) if base else spread * noise
        out[name] = jnp.asarray(drawn.astype(out[name].dtype))
    for name, factor in factors.items():
        out[name] = (out[name] * factor).astype(out[name].dtype)
    return out
```

```python
from contextlib import ExitStack

import concourse.bass as bass
import numpy as np
from concourse import mybir

F32 = mybir.dt.float32
F32R = mybir.dt.float32r
ALU = mybir.AluOpType
ACT = mybir.ActivationFunctionType
AX_X = mybir.AxisListType.X

B, IMG_H, IMG_W, C = 2, 64, 48, 512
HEADS, D = 8, 64
S = IMG_H * IMG_W
NIT = B * HEADS
CB = 16
NCB = IMG_W // CB
TR = 128 // CB
NA = IMG_H // TR
KU = S // NCB
GT = 4
GQ = GT * 128
NG = S // GQ
NU = GT * NCB
NJ = S // 128
NSTEP = NJ // 2
UR = 2 * IMG_H - TR
CT = C // 128
TT = 512
NTT = S // TT
NORM_G = 16
EPS = 1e-5
SCALE = D ** -0.5
LOWEST = float(np.finfo(np.float32).min)
NM = 12

UNIT_STEP = [0, 0, 1, 2, 3, 4, 5, 5, 6, 7, 8, 9]
ACT_ODD = (2, 7)
ACT_CHUNKS = [j for j in range(NJ) if j % 2 == 0 or j // 2 in ACT_ODD]
DVE_CHUNKS = [j for j in range(NJ) if j not in ACT_CHUNKS]
SUM_STEP, BC_STEP, BC_COPY_STEP = 3, 6, 8


def exp_pieces(step):
    out = []
    for t in range(GT):
        last = UNIT_STEP[3 * t + 2]
        out += [(t, c) for c, s in ((0, last + 1), (1, last + 1), (2, last + 2)) if s == step]
    return out


def attention_kernel(nc, xT, w_qkv, w_out, row_win, col_win, ident_in, avg_in, outT):
    with ExitStack() as ctx:
        def sb(name, shape, dt=F32):
            return ctx.enter_context(nc.sbuf_tensor(name, shape, dt))

        def sem(name):
            return ctx.enter_context(nc.semaphore(name))

        q_dram = nc.dram_tensor("q_scratch", [NIT, 2, D, S], F32).ap()
        k_dram = nc.dram_tensor("k_scratch", [NIT, 2, D, S], F32).ap()
        v_dram = nc.dram_tensor("v_scratch", [NIT, S, D], F32).ap()
        o_dram = nc.dram_tensor("o_scratch", [NIT, D, S], F32).ap()

        ring = sb("ring", [128, 2 * GT, S])
        bias = sb("bias", [128, NCB, NCB, UR * CB])
        k_hl = sb("k_hl", [128, S], F32R)
        q_hl = sb("q_hl", [128, 2, 2, GQ], F32R)
        v_sb = sb("v_sb", [128, NJ, D])
        pT = sb("pT", [128, 4, GQ])
        diag = sb("diag", [128, GT, 128])
        ident = sb("ident", [128, 128])
        ones = sb("ones", [128, D])
        row_t = sb("row_t", [128, UR])
        col_t = sb("col_t", [128, NCB, NCB, CB])
        o_half = sb("o_half", [D, GQ])
        o_out = sb("o_out", [D, GQ])
        inv_bc = sb("inv_bc", [D, GQ])
        maxes = sb("maxes", [128, 2 * GT, NCB])
        neg_max = sb("neg_max", [128, 2 * GT])
        sums = sb("sums", [128, 2 * GT, NCB])
        sum_t = sb("sum_t", [128, GT])
        inv_t = sb("inv_t", [128, GT])
        spare = diag.rearrange("p t n -> p (t n)")
        avg = spare[:, 0:128]
        bn = spare[:, 128:128 + NTT * 6].rearrange("p (k s) -> p k s", s=6)
        mv = spare[:, 192:192 + B * CT * 2].rearrange("p (i s) -> p i s", s=2)
        stat = spare[:, 256:256 + 9 * B * CT].rearrange("p (s i) -> p s i", i=B * CT)
        flat = bias.rearrange("p a b c -> p (a b c)")
        w_sb = flat[:, 0:CT * 3 * C].rearrange("p (c n) -> p c n", c=CT)
        xn = flat[:, CT * 3 * C:CT * 3 * C + 2 * CT * TT].rearrange("p (b c n) -> p b c n", b=2, c=CT)

        ps = ctx.enter_context(nc.psum_tensor("ps", [128, 8, 512], F32))
        ps_s = [ps[:, 0:2, :], ps[:, 2:4, :]]
        ps_t = [ps[:, 4, :], ps[:, 5, :]]
        ps_o = [ps[:, 6, :], ps[:, 7, :]]

        x_loaded = [sem(f"x_loaded{i}") for i in range(B * CT)]
        consts_loaded = sem("consts_loaded")
        w_loaded = sem("w_loaded")
        stats_step = sem("stats_step")
        group_avg = sem("group_avg")
        root_done = sem("root_done")
        xn_ready = sem("xn_ready")
        proj_done = sem("proj_done")
        hi_done = sem("hi_done")
        lo_done = sem("lo_done")
        v_done = sem("v_done")
        qk_stored = [sem(f"qk_stored{i}") for i in range(4)]
        v_stored = [sem(f"v_stored{i}") for i in range(4)]

        ones_set = sem("ones_set")
        tables_loaded = sem("tables_loaded")
        bias_ready = sem("bias_ready")
        k_loaded = sem("k_loaded")
        v_loaded = sem("v_loaded")
        q_loaded = [sem("q_loaded0"), sem("q_loaded1")]
        scores_ready = sem("scores_ready")
        biased = sem("biased")
        negmax_ready = sem("negmax_ready")
        exp_done = sem("exp_done")
        transposed = sem("transposed")
        pT_act = sem("pT_act")
        pT_dve = sem("pT_dve")
        o_ready = sem("o_ready")
        half_ready = sem("half_ready")
        o_summed = sem("o_summed")
        o_scaled = sem("o_scaled")
        o_stored = sem("o_stored")
        sums_ready = sem("sums_ready")
        inv_ready = sem("inv_ready")
        diag_ready = sem("diag_ready")
        bc_ready = sem("bc_ready")
        bc_copied = sem("bc_copied")

        wo_loaded = sem("wo_loaded")
        in_loaded = [sem("in_loaded0"), sem("in_loaded1")]
        out_proj = sem("out_proj")
        out_added = sem("out_added")
        out_stored = [sem("out_stored0"), sem("out_stored1")]

        o_in = [ring[:, b, 0:CT * TT].rearrange("p (c n) -> p c n", c=CT) for b in range(2)]
        x_in = [ring[:, 2 + b, 0:CT * TT].rearrange("p (c n) -> p c n", c=CT) for b in range(2)]
        y_out = [ring[:, 4 + b, 0:CT * TT].rearrange("p (c n) -> p c n", c=CT) for b in range(2)]
        wo_sb = ring[:, 6, 0:CT * C].rearrange("p (c n) -> p c n", c=CT)

        def qk_stage(s):
            if s < 2:
                return k_hl[:, s * 2 * TT:(s + 1) * 2 * TT].rearrange("p (h n) -> p h n", h=2)
            return q_hl[:, s - 2]

        block = ctx.enter_context(nc.Block())

        PROJ0, LO0, V0, QKST0, VST0 = 24, 8, 4, 32, 16
        OSC0, OST0, BCC0, PTA0, PTD0, OADD0 = 1, 16, 1, 1, 1, CT * B

        @block.sync
        def _(sp):
            for b in range(B):
                for c in range(CT):
                    sp.dma_start(ring[:, b * CT + c, :], xT[b, c * 128:(c + 1) * 128, :]).then_inc(
                        x_loaded[b * CT + c], 16)
            sp.dma_start(avg, avg_in).then_inc(consts_loaded, 16)
            sp.dma_start(ident[:], ident_in).then_inc(consts_loaded, 16)
            sp.dma_start(w_sb, w_qkv.rearrange("(c p) n -> p c n", p=128)).then_inc(w_loaded, 16)
            sp.dma_start(row_t[:], row_win[0]).then_inc(tables_loaded, 16)
            sp.dma_start(col_t[:], col_win[0]).then_inc(tables_loaded, 16)

            with sp.Fori(0, NTT) as i:
                for b in range(B):
                    n = 2 * i + b
                    tok = bass.ds(i * TT, TT)
                    for m in range(8):
                        sp.wait_ge(lo_done, LO0 + 8 * n + m + 1)
                        dram = q_dram if m < 4 else k_dram
                        for hh in range(2):
                            sp.dma_start(
                                dram[b * HEADS + 2 * (m % 4) + hh, :, :, tok].rearrange("l d n -> d l n"),
                                qk_stage(m % 4)[hh * D:(hh + 1) * D].bitcast(F32),
                            ).then_inc(qk_stored[m % 4], 16)
                    for s in range(4):
                        sp.wait_ge(v_done, V0 + 4 * n + s + 1)
                        sp.dma_start(
                            v_dram[b * HEADS:(b + 1) * HEADS, bass.ds(i * TT + s * 128, 128), :].rearrange(
                                "h t d -> t h d"),
                            pT[:, s, :].rearrange("p (h d) -> p h d", h=HEADS),
                        ).then_inc(v_stored[s], 16)

            def all_projected(eng):
                for s in range(4):
                    eng.wait_ge(qk_stored[s], QKST0 + 32 * 2 * B * NTT)
                    eng.wait_ge(v_stored[s], VST0 + 16 * B * NTT)

            def load_k(it):
                sp.dma_start(k_hl[:].bitcast(F32), k_dram[it].rearrange("l d n -> (l d) n")).then_inc(k_loaded, 16)

            def load_v(it):
                sp.dma_start(v_sb[:], v_dram[it].rearrange("(j p) d -> p j d", p=128)).then_inc(v_loaded, 16)

            def load_q(it, g):
                src = q_dram[it, :, :, g * GQ:(g + 1) * GQ].rearrange("l d n -> d l n")
                for half in range(2):
                    sp.dma_start(q_hl[half * D:(half + 1) * D, g % 2].bitcast(F32), src).then_inc(q_loaded[g % 2], 16)

            def store_o(it, g):
                sp.wait_ge(o_scaled, OSC0 + it * NG + g + 1)
                sp.dma_start(o_dram[it, :, g * GQ:(g + 1) * GQ], o_out[:]).then_inc(o_stored, 16)

            all_projected(sp)
            load_k(0)
            load_q(0, 0)
            load_q(0, 1)
            load_v(0)

            def head(it, last):
                for g in range(NG):
                    G = it * NG + g
                    if g == 0 and not last:
                        sp.wait_ge(bias_ready, NCB * (it + 1))
                        sp.dma_start(row_t[:], row_win[it + 1]).then_inc(tables_loaded, 16)
                        sp.dma_start(col_t[:], col_win[it + 1]).then_inc(tables_loaded, 16)
                    sp.wait_ge(scores_ready, NU * (G + 1))
                    if g == NG - 1 and not last:
                        load_k(it + 1)
                    if g + 2 < NG:
                        load_q(it, g + 2)
                    elif not last:
                        load_q(it + 1, g + 2 - NG)
                    if g > 0:
                        store_o(it, g - 1)
                if not last:
                    sp.wait_ge(o_ready, (it + 1) * NG)
                    load_v(it + 1)
                store_o(it, NG - 1)

            with sp.Fori(0, NIT - 1) as it:
                head(it, False)
            head(NIT - 1, True)

            sp.wait_ge(o_stored, OST0 + 16 * NIT * NG)
            sp.dma_start(wo_sb, w_out.rearrange("(c p) n -> p c n", p=128)).then_inc(wo_loaded, 16)

            def load_tile(i, b):
                tok = bass.ds(i * TT, TT)
                for c in range(CT):
                    sp.dma_start(o_in[b][:, c, :], o_dram[b * HEADS + 2 * c:b * HEADS + 2 * c + 2, :, tok]
                                 .rearrange("h d n -> (h d) n")).then_inc(in_loaded[b], 16)
                sp.dma_start(x_in[b], xT[b, :, tok].rearrange("(c p) n -> p c n", p=128)).then_inc(
                    in_loaded[b], 16)

            load_tile(0, 0)
            load_tile(0, 1)

            def tile_out(i, last):
                for b in range(B):
                    sp.wait_ge(out_added, OADD0 + CT * (B * i + b + 1))
                    sp.dma_start(outT[b, :, bass.ds(i * TT, TT)].rearrange("(c p) n -> p c n", p=128),
                                 y_out[b]).then_inc(out_stored[b], 16)
                    if not last:
                        load_tile(i + 1, b)

            with sp.Fori(0, NTT - 1) as i:
                tile_out(i, False)
            tile_out(NTT - 1, True)
            for b in range(B):
                sp.wait_ge(out_stored[b], 16 * NTT + 16)

        @block.tensor
        def _(pe):
            pe.wait_ge(consts_loaded, 32)
            pe.wait_ge(stats_step, 1)
            nc.tensor.matmul(ps[:, 0, 0:B * CT], avg, stat[:, 0, :], start=True, stop=True).then_inc(
                group_avg, 1)
            pe.wait_ge(stats_step, 2)
            nc.tensor.matmul(ps[:, 0, 0:B * CT], avg, stat[:, 1, :], start=True, stop=True).then_inc(
                group_avg, 1)

            pe.wait_ge(w_loaded, 16)
            pe.wait_ge(stats_step, 3)
            with pe.Fori(0, NTT) as i:
                for b in range(B):
                    n = 2 * i + b
                    pe.wait_ge(xn_ready, n + 1)
                    for m in range(NM):
                        was = m - 8 if m >= 8 else m + 4
                        before = n if m >= 8 else n - 1
                        if was < 8:
                            pe.wait_ge(lo_done, LO0 + 8 * before + was + 1)
                        else:
                            pe.wait_ge(v_done, V0 + 4 * before + was - 8 + 1)
                        bank = ps[:, (b * NM + m) % 8, :]
                        for c in range(CT):
                            if m < 8:
                                mm = nc.tensor.matmul(bank, w_sb[:, c, m * 128:(m + 1) * 128], xn[:, b, c, :],
                                                      start=(c == 0), stop=(c == CT - 1))
                            else:
                                mm = nc.tensor.matmul(bank, xn[:, b, c, (m - 8) * 128:(m - 7) * 128],
                                                      w_sb[:, c, 2 * C:3 * C],
                                                      start=(c == 0), stop=(c == CT - 1))
                        mm.then_inc(proj_done, 1)

            pe.wait_ge(lo_done, LO0 + 8 * B * NTT)
            pe.wait_ge(v_done, V0 + 4 * B * NTT)
            pe.wait_ge(ones_set, 1)

            def score_unit(it, g, u):
                G, t, c = it * NG + g, u // NCB, u % NCB
                U = NU * G + u
                if u == 0:
                    pe.wait_ge(q_loaded[g % 2], 32 * ((NG // 2) * it + g // 2 + 1))
                    if g == 0:
                        pe.wait_ge(k_loaded, 16 * (it + 1))
                if not (isinstance(U, int) and U < 2):
                    pe.wait_ge(biased, U - 1)
                for part in range(2):
                    for half in range(2):
                        mm = nc.tensor.matmul(
                            ps_s[u % 2][:, half, :], q_hl[:, g % 2, part, t * 128:(t + 1) * 128],
                            k_hl[:, c * KU + half * 512:c * KU + (half + 1) * 512],
                            start=(part == 0), stop=(part == 1))
                mm.then_inc(scores_ready, 1)

            def evacuated(it, g, j):
                G = it * NG + g
                if j in ACT_CHUNKS:
                    pe.wait_ge(pT_act, PTA0 + len(ACT_CHUNKS) * G + ACT_CHUNKS.index(j) + 1)
                else:
                    pe.wait_ge(pT_dve, PTD0 + len(DVE_CHUNKS) * G + DVE_CHUNKS.index(j) + 1)

            def transposes(it, g, j):
                G = it * NG + g
                if j % 8 == 0:
                    pe.wait_ge(exp_done, NU * G + NU - NCB + j // 8 + 1)
                if j >= 2:
                    evacuated(it, g, j - 2)
                else:
                    evacuated(it, g - 1, NJ + j - 2)
                for t in range(GT):
                    mm = nc.tensor.transpose(ps_t[j % 2][:, t * 128:(t + 1) * 128],
                                             ring[:, (g % 2) * GT + t, j * 128:(j + 1) * 128], ident[:])
                mm.then_inc(transposed, 1)

            def products(it, g, pair):
                G = it * NG + g
                if pair == 0:
                    pe.wait_ge(bc_copied, BCC0 + G)
                    if g == 0:
                        pe.wait_ge(v_loaded, 16 * (it + 1))
                for j in (2 * pair, 2 * pair + 1):
                    evacuated(it, g, j)
                for j in (2 * pair, 2 * pair + 1):
                    o = (j % 2) * D
                    mm = nc.tensor.matmul(ps_o[g % 2][o:o + D, :], v_sb[:, j, :], pT[:, j % 4, :],
                                          start=(pair == 0), stop=(pair == NSTEP - 1))
                if pair == NSTEP - 1:
                    mm.then_inc(o_ready, 1)

            for u in range(NU):
                score_unit(0, 0, u)

            def head(it, last):
                for g in range(NG):
                    G = it * NG + g
                    nxt = (it, g + 1) if g + 1 < NG else (it + 1, 0)
                    for step in range(NSTEP):
                        transposes(it, g, 2 * step)
                        transposes(it, g, 2 * step + 1)
                        if not (last and g == NG - 1):
                            for u in range(NU):
                                if UNIT_STEP[u] == step:
                                    score_unit(*nxt, u)
                        if step == BC_STEP:
                            pe.wait_ge(diag_ready, G + 1)
                            pe.wait_ge(o_scaled, OSC0 + G)
                            nc.tensor.matmul(ps_o[(g + 1) % 2][0:D, :], ones[:],
                                             diag.rearrange("p t n -> p (t n)"),
                                             start=True, stop=True).then_inc(bc_ready, 1)
                        if step > 0:
                            products(it, g, step - 1)
                        elif g > 0:
                            products(it, g - 1, NSTEP - 1)
                products(it, NG - 1, NSTEP - 1)

            with pe.Fori(0, NIT - 1) as it:
                head(it, False)
            head(NIT - 1, True)

            pe.wait_ge(wo_loaded, 16)
            pe.wait_ge(o_scaled, OSC0 + NIT * NG)
            with pe.Fori(0, NTT) as i:
                for b in range(B):
                    pe.wait_ge(in_loaded[b], 16 * (CT + 1) * (i + 1))
                    pe.wait_ge(out_added, OADD0 + CT * (B * (i - 1) + b + 1))
                    for m in range(CT):
                        for c in range(CT):
                            mm = nc.tensor.matmul(ps[:, b * CT + m, :], wo_sb[:, c, m * 128:(m + 1) * 128],
                                                  o_in[b][:, c, :], start=(c == 0), stop=(c == CT - 1))
                        mm.then_inc(out_proj, 1)

        @block.scalar
        def _(act):
            act.wait_ge(stats_step, 3)
            nc.scalar.activation(stat[:, 3, :], stat[:, 2, :], ACT.Sqrt).then_inc(root_done, 1)

            with act.Fori(0, NTT) as i:
                for b in range(B):
                    n = 2 * i + b
                    for m in range(NM):
                        act.wait_ge(proj_done, PROJ0 + NM * n + m + 1)
                        bank = ps[:, (b * NM + m) % 8, :]
                        if m < 8:
                            act.wait_ge(qk_stored[m % 4], QKST0 + 32 * (2 * n + m // 4))
                            nc.scalar.activation(qk_stage(m % 4)[:, 0, :], bank, ACT.Copy,
                                                 scale=SCALE if m < 4 else 1.0).then_inc(hi_done, 1)
                        else:
                            act.wait_ge(v_stored[m - 8], VST0 + 16 * n)
                            nc.scalar.activation(pT[:, m - 8, :], bank, ACT.Copy).then_inc(v_done, 1)

            for s in range(4):
                act.wait_ge(v_stored[s], VST0 + 16 * B * NTT)

            def exp(it, g, t, c):
                slot = (g % 2) * GT + t
                if c == 0:
                    act.wait_ge(negmax_ready, GT * (it * NG + g) + t + 1)
                p = ring[:, slot, c * KU:(c + 1) * KU]
                nc.scalar.activation(p, p, ACT.Exp, bias=neg_max[:, slot:slot + 1],
                                     accum_out=sums[:, slot, c:c + 1]).then_inc(exp_done, 1)

            def evacuate(it, g, j):
                act.wait_ge(transposed, NJ * (it * NG + g) + j + 1)
                nc.scalar.activation(pT[:, j % 4, :], ps_t[j % 2], ACT.Copy).then_inc(pT_act, 1)

            def half(it, g):
                act.wait_ge(o_ready, it * NG + g + 1)
                nc.scalar.activation(o_half[:], ps_o[g % 2][D:2 * D, :], ACT.Copy).then_inc(half_ready, 1)

            for t in range(GT):
                for c in range(NCB):
                    exp(0, 0, t, c)

            def head(it, last):
                for g in range(NG):
                    nxt = (it, g + 1) if g + 1 < NG else (it + 1, 0)
                    for step in range(NSTEP):
                        for j in (2 * step, 2 * step + 1):
                            if j in ACT_CHUNKS:
                                evacuate(it, g, j)
                        if step == 0 and g > 0:
                            half(it, g - 1)
                        if step == BC_COPY_STEP:
                            act.wait_ge(bc_ready, it * NG + g + 1)
                            nc.scalar.activation(inv_bc[:], ps_o[(g + 1) % 2][0:D, :], ACT.Copy).then_inc(
                                bc_copied, 1)
                        if not (last and g == NG - 1):
                            for t, c in exp_pieces(step):
                                exp(*nxt, t, c)
                half(it, NG - 1)

            with act.Fori(0, NIT - 1) as it:
                head(it, False)
            head(NIT - 1, True)

        @block.gpsimd
        def _(pool):
            nc.gpsimd.memset(ones[:], 1.0).then_inc(ones_set, 1)
            group_reg = pool.alloc_register("groups")
            pool.reg_mov(group_reg, 0)

            def build_bias(it, cb):
                if cb == 0:
                    pool.wait_ge(tables_loaded, 32 * (it + 1))
                for kb in range(NCB):
                    op = nc.gpsimd.tensor_tensor(
                        bias[:, cb, kb, :].rearrange("p (u j) -> p u j", j=CB),
                        row_t[:].unsqueeze(2).to_broadcast([128, UR, CB]),
                        col_t[:, cb, kb, :].unsqueeze(1).to_broadcast([128, UR, CB]), ALU.add)
                op.then_inc(bias_ready, 1)

            def diagonals(it, g):
                pool.reg_add(group_reg, group_reg, 1)
                pool.wait_ge(consts_loaded, 32)
                pool.wait_ge(inv_ready, group_reg)
                for t in range(GT):
                    op = nc.gpsimd.tensor_scalar(diag[:, t, :], ident[:], inv_t[:, t:t + 1], None, ALU.mult)
                op.then_inc(diag_ready, 1)

            pool.wait_ge(consts_loaded, 32)
            pool.wait_ge(proj_done, PROJ0 + NM * B * NTT)
            for cb in range(NCB):
                build_bias(0, cb)

            def head(it, last):
                for g in range(NG):
                    diagonals(it, g)
                    if g % 2 == 1 and not last:
                        pool.wait_ge(biased, NU * (it * NG + g + 1))
                        build_bias(it + 1, g // 2)

            with pool.Fori(0, NIT - 1) as it:
                head(it, False)
            head(NIT - 1, True)

        @block.vector
        def _(dve):
            unit_reg = dve.alloc_register("units")
            dve.reg_mov(unit_reg, 0)
            for s, value in ((proj_done, PROJ0), (lo_done, LO0), (v_done, V0), (o_scaled, OSC0),
                             (o_stored, OST0), (bc_copied, BCC0), (pT_act, PTA0), (pT_dve, PTD0), (out_added, OADD0),
                             *((q, QKST0) for q in qk_stored), *((q, VST0) for q in v_stored),
                             *((q, 16) for q in out_stored)):
                dve.sem_inc(s, value)

            own = sem("stats_own")
            own_n = 0
            for i in range(B * CT):
                dve.wait_ge(x_loaded[i], 16)
                for k in range(NTT):
                    op = nc.vector.bn_stats(bn[:, k, :], ring[:, i, k * TT:(k + 1) * TT])
                op.then_inc(own, 1)
                own_n += 1
                dve.wait_ge(own, own_n)
                nc.vector.bn_aggr(mv[:, i, :], bn).then_inc(own, 1)
                own_n += 1
                dve.wait_ge(own, own_n)
            nc.vector.tensor_copy(stat[:, 0, :], mv[:, :, 0]).then_inc(stats_step, 1)
            dve.wait_ge(group_avg, 1)
            nc.vector.tensor_copy(stat[:, 4, :], ps[:, 0, 0:B * CT]).then_inc(own, 1)
            dve.wait_ge(own, own_n + 1)
            nc.vector.tensor_tensor(stat[:, 5, :], stat[:, 0, :], stat[:, 4, :], ALU.subtract).then_inc(own, 1)
            dve.wait_ge(own, own_n + 2)
            nc.vector.tensor_tensor(stat[:, 6, :], stat[:, 5, :], stat[:, 5, :], ALU.mult).then_inc(own, 1)
            dve.wait_ge(own, own_n + 3)
            nc.vector.tensor_tensor(stat[:, 1, :], stat[:, 6, :], mv[:, :, 1], ALU.add).then_inc(stats_step, 1)
            dve.wait_ge(group_avg, 2)
            nc.vector.tensor_scalar(stat[:, 2, :], ps[:, 0, 0:B * CT], EPS, None, ALU.add).then_inc(stats_step, 1)
            dve.wait_ge(root_done, 1)
            nc.vector.reciprocal(stat[:, 5, :], stat[:, 3, :]).then_inc(own, 1)
            dve.wait_ge(own, own_n + 4)
            nc.vector.tensor_tensor(stat[:, 6, :], stat[:, 2, :], stat[:, 5, :], ALU.mult).then_inc(own, 1)
            dve.wait_ge(own, own_n + 5)
            nc.vector.tensor_tensor(stat[:, 7, :], stat[:, 6, :], stat[:, 3, :], ALU.add).then_inc(own, 1)
            dve.wait_ge(own, own_n + 6)
            nc.vector.tensor_scalar(stat[:, 7, :], stat[:, 7, :], 0.5, None, ALU.mult).then_inc(own, 1)
            dve.wait_ge(own, own_n + 7)
            nc.vector.reciprocal(stat[:, 8, :], stat[:, 7, :]).then_inc(own, 1)
            dve.wait_ge(own, own_n + 8)

            def normalise(i, b):
                dve.wait_ge(proj_done, PROJ0 + NM * (2 * i + b - 1))
                for c in range(CT):
                    k = b * CT + c
                    op = nc.vector.tensor_scalar(xn[:, b, c, :], ring[:, k, bass.ds(i * TT, TT)],
                                                 stat[:, 4, k:k + 1], stat[:, 8, k:k + 1],
                                                 ALU.subtract, ALU.mult)
                op.then_inc(xn_ready, 1)

            with dve.Fori(0, NTT) as i:
                for b in range(B):
                    n = 2 * i + b
                    normalise(i, b)
                    for m in range(8):
                        dve.wait_ge(hi_done, 8 * n + m + 1)
                        stage = qk_stage(m % 4)
                        nc.vector.scalar_tensor_tensor(
                            out=stage[:, 1, :], in0=ps[:, (b * NM + m) % 8, :], scalar=SCALE if m < 4 else 1.0,
                            in1=stage[:, 0, :].bitcast(F32), op0=ALU.mult, op1=ALU.subtract).then_inc(lo_done, 1)

            for s in range(4):
                dve.wait_ge(v_stored[s], VST0 + 16 * B * NTT)

            def bias_unit(it, g, u):
                G, t, c = it * NG + g, u // NCB, u % NCB
                U = NU * G + u
                slot, tile = (g % 2) * GT + t, g * GT + t
                cb, a = tile // NA, tile % NA
                if g % 2 == 0 and u == 0:
                    dve.wait_ge(bias_ready, NCB * it + cb + 1)
                dve.reg_add(unit_reg, unit_reg, 1)
                dve.wait_ge(stats_step, 3)
                dve.wait_ge(scores_ready, unit_reg)
                first = (IMG_H - TR - TR * a) * CB
                nc.vector.tensor_tensor_reduce(
                    out=ring[:, slot, c * KU:(c + 1) * KU], in0=ps_s[u % 2].rearrange("p a n -> p (a n)"),
                    in1=bias[:, cb, c, first:first + KU], scale=1.0, scalar=LOWEST,
                    op0=ALU.add, op1=ALU.max, accum_out=maxes[:, slot, c:c + 1]).then_inc(biased, 1)
                if c == NCB - 1:
                    dve.wait_ge(biased, U + 1)
                    nc.vector.tensor_reduce(neg_max[:, slot:slot + 1], maxes[:, slot, :], AX_X, ALU.max,
                                            negate=True).then_inc(negmax_ready, 1)

            def evacuate(it, g, j):
                dve.wait_ge(transposed, NJ * (it * NG + g) + j + 1)
                nc.vector.tensor_copy(pT[:, j % 4, :], ps_t[j % 2]).then_inc(pT_dve, 1)

            def inverse_sums(it, g):
                G = it * NG + g
                dve.wait_ge(exp_done, NU * (G + 1))
                nc.vector.tensor_reduce(sum_t[:], sums[:, (g % 2) * GT:(g % 2 + 1) * GT, :], AX_X,
                                        ALU.add).then_inc(sums_ready, 1)
                dve.wait_ge(sums_ready, G + 1)
                nc.vector.reciprocal(inv_t[:], sum_t[:]).then_inc(inv_ready, 1)

            def output(it, g):
                G = it * NG + g
                dve.wait_ge(half_ready, G + 1)
                nc.vector.tensor_tensor(o_half[:], ps_o[g % 2][0:D, :], o_half[:], ALU.add).then_inc(o_summed, 1)
                dve.wait_ge(o_summed, G + 1)
                dve.wait_ge(bc_copied, BCC0 + G + 1)
                dve.wait_ge(o_stored, OST0 + 16 * G)
                nc.vector.tensor_tensor(o_out[:], o_half[:], inv_bc[:], ALU.mult).then_inc(o_scaled, 1)

            for u in range(NU):
                bias_unit(0, 0, u)

            def head(it, last):
                for g in range(NG):
                    nxt = (it, g + 1) if g + 1 < NG else (it + 1, 0)
                    for step in range(NSTEP):
                        j = 2 * step + 1
                        if j in DVE_CHUNKS:
                            evacuate(it, g, j)
                        if not (last and g == NG - 1):
                            for u in range(NU):
                                if UNIT_STEP[u] == step:
                                    bias_unit(*nxt, u)
                        if step == 1 and g > 0:
                            output(it, g - 1)
                        if step == SUM_STEP:
                            inverse_sums(it, g)
                output(it, NG - 1)

            with dve.Fori(0, NIT - 1) as it:
                head(it, False)
            head(NIT - 1, True)

            with dve.Fori(0, NTT) as i:
                for b in range(B):
                    dve.wait_ge(out_stored[b], 16 * i + 16)
                    dve.wait_ge(in_loaded[b], 16 * (CT + 1) * (i + 1))
                    for m in range(CT):
                        dve.wait_ge(out_proj, CT * (B * i + b) + m + 1)
                        nc.vector.tensor_tensor(y_out[b][:, m, :], ps[:, b * CT + m, :], x_in[b][:, m, :],
                                                ALU.add).then_inc(out_added, 1)


def kernel(x, L0_conv_w_qkv, L0_conv_w_out, L0_conv_rel_row_tab, L0_conv_rel_col_tab):
    from concourse import bacc
    from concourse.bass_utils import run_bass_kernel_spmd

    xT = np.asarray(x).reshape(B, IMG_H, NCB, CB, C).transpose(0, 4, 2, 1, 3).reshape(B, C, S)
    p = np.arange(128)
    row_at = (p // CB)[:, None] - np.arange(UR)[None, :] + (IMG_H - TR) + IMG_H - 1
    blocks = np.arange(NCB) * CB
    col_at = ((p % CB)[:, None, None, None] + blocks[None, :, None, None] - blocks[None, None, :, None]
              - np.arange(CB)[None, None, None, :] + IMG_W - 1)
    row_win = np.tile(np.asarray(L0_conv_rel_row_tab).T[:, row_at], (B, 1, 1))
    col_win = np.tile(np.asarray(L0_conv_rel_col_tab).T[:, col_at], (B, 1, 1, 1, 1))
    group = np.arange(128) // NORM_G
    arrays = {
        "xT": xT, "w_qkv": np.asarray(L0_conv_w_qkv), "w_out": np.asarray(L0_conv_w_out),
        "row_win": row_win, "col_win": col_win, "ident": np.eye(128, dtype=np.float32),
        "avg": ((group[:, None] == group[None, :]) / NORM_G).astype(np.float32),
    }
    arrays = {f"in_{k}": np.ascontiguousarray(v) for k, v in arrays.items()}
    nc = bacc.Bacc("TRN2", target_bir_lowering=False, num_devices=1)
    aps = [nc.dram_tensor(k, v.shape, mybir.dt.from_np(v.dtype), kind="ExternalInput").ap()
           for k, v in arrays.items()]
    out = nc.dram_tensor("outT", (B, C, S), F32, kind="ExternalOutput").ap()
    attention_kernel(nc, *aps, out)
    result = run_bass_kernel_spmd(nc, [arrays], core_ids=[0]).results[0]["outT"]
    return np.ascontiguousarray(
        result.reshape(B, C, NCB, IMG_H, CB).transpose(0, 3, 2, 4, 1).reshape(B, IMG_H, IMG_W, C))
```

```python
from contextlib import ExitStack

import concourse.bass as bass
import numpy as np
from concourse import mybir

F32 = mybir.dt.float32
F32R = mybir.dt.float32r
BF16 = mybir.dt.bfloat16
ALU = mybir.AluOpType
ACT = mybir.ActivationFunctionType
AX_X = mybir.AxisListType.X

B, IMG_H, IMG_W, C = 2, 64, 48, 512
HEADS, D = 8, 64
S = IMG_H * IMG_W
NIT = B * HEADS
CB = 16
NCB = IMG_W // CB
TR = 128 // CB
NA = IMG_H // TR
KU = S // NCB
GT = 4
GQ = GT * 128
NG = S // GQ
NU = GT * NCB
NP = S // 256
UR = 2 * IMG_H - TR
QB = 16
NQB = GQ // (QB * CB)
WR = 2 * IMG_H - QB
ND = 2 * NCB - 1
MROWS = 1 + 2 * (QB + CB - 1)
KB = D + MROWS
CT = C // 128
TT = 512
NTT = S // TT
NORM_G = 16
EPS = 1e-5
SCALE = D ** -0.5
LOWEST = float(np.finfo(np.float32).min)
NM = 12

UNIT_STEP = [0, 1, 1, 3, 3, 4, 5, 6, 6, 8, 8, 9]
PT = 4
FILLS = [f for s in range(NP) for f in [("S", s)] + [("M", u) for u in range(NU) if UNIT_STEP[u] == s]]
NSLOT = 3
assert len(FILLS) % NSLOT == 0 and NU % NSLOT == 0
HALF_STEP, ADD_STEP, MERGE_STEP, SUM_STEP, INV_STEP, DIAG_STEP, BC_STEP, OUT_STEP = 1, 1, 2, 3, 4, 5, 6, 7
TABLE_STEPS = [3, 4, 5, 6, 7, 8]
BUILDS = {
    (0, 1): ("E", 2, 0, 0), (0, 6): ("R", 0, 0), (0, 8): ("E", 2, 1, 0),
    (1, 1): ("E", 2, 2, 0),
    (2, 1): ("E", 0, 0, 1), (2, 6): ("R", 4, 1), (2, 8): ("E", 0, 1, 1),
    (3, 1): ("E", 0, 2, 1), (3, 6): ("R", 3, 1), (3, 8): ("E", 1, 0, 1),
    (4, 1): ("E", 1, 1, 1), (4, 6): ("R", 2, 1),
    (5, 1): ("E", 1, 2, 1), (5, 6): ("R", 1, 1),
}
ROW_BUILDS = [(g, what[1], what[2]) for (g, s), what in BUILDS.items() if what[0] == "R"]
HI_STEP, LO_STEPS = 9, (10, 11)
FIRST_ROWS = (2, 3, 4, 1)


def user_before(k, present):
    back, k = 0, k - NSLOT
    while True:
        if k < 0:
            back, k = back + 1, k + len(FILLS)
        if back or present(FILLS[k]):
            return back, FILLS[k]
        k -= NSLOT


def attention_kernel(nc, xT, w_qkv, w_out, row_win, col_win, row_rows, col_rows, col_less, neg_lo,
                     onehots, ident_in, avg_in, outT):
    with ExitStack() as ctx:
        def sb(name, shape, dt=F32, stack=ctx):
            return stack.enter_context(nc.sbuf_tensor(name, shape, dt))

        def sem(name):
            return ctx.enter_context(nc.semaphore(name))

        q_dram = nc.dram_tensor("q_scratch", [NIT, 2, D, S], F32).ap()
        k_dram = nc.dram_tensor("k_scratch", [NIT, 2, D, S], F32).ap()
        v_dram = nc.dram_tensor("v_scratch", [NIT, S, D], F32).ap()
        o_dram = nc.dram_tensor("o_scratch", [NIT, D, S], F32).ap()

        ident = sb("ident", [128, 128])

        with ExitStack() as one:
            x_sb = sb("x_sb", [128, B * CT, S], F32, one)
            w_hi = sb("w_hi", [128, CT, 3 * C], F32R, one)
            w_lo = sb("w_lo", [128, CT, 3 * C], F32R, one)
            x_hi = sb("x_hi", [128, 2, CT, TT], F32R, one)
            x_lo = sb("x_lo", [128, 2, CT, TT], F32R, one)
            qk_stage = sb("qk_stage", [128, 4, 2, TT], F32R, one)
            v_stage = sb("v_stage", [128, 4, TT], F32, one)
            small = sb("small", [128, 336], F32, one)
            avg = small[:, 0:128]
            bn = small[:, 128:128 + NTT * 6].rearrange("p (k s) -> p k s", s=6)
            mv = small[:, 192:192 + B * CT * 2].rearrange("p (i s) -> p i s", s=2)
            stat = small[:, 256:256 + 9 * B * CT].rearrange("p (s i) -> p s i", i=B * CT)
        w_raw = v_stage.rearrange("p a n -> p (a n)")[:, 0:3 * C]
        with ExitStack() as two:
            bias = sb("bias", [128, NCB, NCB, UR * CB], BF16, two)
            rows = sb("rows", [128, ND, WR * CB], F32R, two)
            rows_sum = sb("rows_sum", [128, WR * CB], F32, two)
            k_mov = sb("k_mov", [128, S], F32R, two)
            k_st = sb("k_st", [128, S], F32R, two)
            k_rows = sb("k_rows", [128, 2, NQB, S], F32R, two)
            q_hi = sb("q_hi", [128, 3, GQ], F32R, two)
            q_rows = sb("q_rows", [128, 2, GQ], F32R, two)
            v_sb = sb("v_sb", [128, S // 128, D], F32, two)
            pT = sb("pT", [128, PT, 2, GQ], F32, two)
            junk = sb("junk", [128, NCB, KU], BF16, two)
            acc_d = sb("acc_d", [128, 2, GQ], F32, two)
            acc_p = sb("acc_p", [128, 2, GQ], F32, two)
            acc = sb("acc", [128, GQ], F32, two)
            diag = sb("diag", [128, GT, 128], F32, two)
            ident_r = sb("ident_r", [128, 128], F32R, two)
            ones = sb("ones", [128, D], F32, two)
            row_t = sb("row_t", [128, UR], F32, two)
            col_t = sb("col_t", [128, NCB, NCB, CB], F32, two)
            rrow_t = sb("rrow_t", [128, WR], F32, two)
            rcol_t = sb("rcol_t", [128, ND, CB], F32, two)
            rless_t = sb("rless_t", [128, ND, CB], F32, two)
            neg_lo_t = sb("neg_lo_t", [128, 1], F32, two)
            o_sum = sb("o_sum", [D, GQ], F32, two)
            o_out = sb("o_out", [D, GQ], F32, two)
            maxes = sb("maxes", [128, 2, GT, NCB], F32, two)
            neg_max = sb("neg_max", [128, 2, GT], F32R, two)
            inv_t = sb("inv_t", [128, GT], F32, two)
        with ExitStack() as three:
            o_in = sb("o_in", [128, 2, CT, TT], F32, three)
            x_in = sb("x_in", [128, 2, CT, TT], F32, three)
            y_out = sb("y_out", [128, 2, CT, TT], F32, three)
            wo_sb = sb("wo_sb", [128, CT, C], F32, three)

        ps = ctx.enter_context(nc.psum_tensor("ps", [128, 8, 512], F32))
        ps_slot = [ps[:, 2 * i:2 * i + 2, :] for i in range(NSLOT)]
        ps_o = ps[:, 6, :]
        ps_x = ps[:, 7, :]

        x_loaded = [sem(f"x_loaded{i}") for i in range(B * CT)]
        consts_loaded = sem("consts_loaded")
        w_loaded = sem("w_loaded")
        w_hi_done = sem("w_hi_done")
        w_lo_done = sem("w_lo_done")
        stats_own = sem("stats_own")
        stats_step = sem("stats_step")
        group_avg = sem("group_avg")
        root_done = sem("root_done")
        x_normed = sem("x_normed")
        x_hi_done = sem("x_hi_done")
        x_lo_done = sem("x_lo_done")
        proj_done = sem("proj_done")
        hi_done = sem("hi_done")
        lo_done = sem("lo_done")
        v_done = sem("v_done")
        qk_stored = [sem(f"qk_stored{i}") for i in range(4)]
        v_stored = [sem(f"v_stored{i}") for i in range(4)]

        ones_set = sem("ones_set")
        onehots_loaded = sem("onehots_loaded")
        onehots_set = sem("onehots_set")
        bias_in = sem("bias_in")
        rows_in = sem("rows_in")
        bias_ready = sem("bias_ready")
        cols_less = sem("cols_less")
        rows_summed = sem("rows_summed")
        rows_rounded = sem("rows_rounded")
        rows_ready = sem("rows_ready")
        k_mov_in = [sem(f"k_mov_in{c}") for c in range(NCB)]
        k_st_in = [sem(f"k_st_in{c}") for c in range(NCB)]
        k_rows_in = [sem(f"k_rows_in{k}") for k in range(2)]
        k_rows_set = sem("k_rows_set")
        q_hi_in = [sem(f"q_hi_in{k}") for k in range(3)]
        q_lo_in = [sem(f"q_lo_in{k}") for k in range(2)]
        v_in = [sem(f"v_in{c}") for c in range(NCB)]
        unit_filled = sem("unit_filled")
        unit_maxed = sem("unit_maxed")
        max_ready = sem("max_ready")
        max_row = sem("max_row")
        max_row_set = sem("max_row_set")
        pair_filled = sem("pair_filled")
        exp_done = sem("exp_done")
        pair_used = sem("pair_used")
        dve_added = sem("dve_added")
        pool_added = sem("pool_added")
        acc_merged = sem("acc_merged")
        acc_ready = sem("acc_ready")
        sums_ready = sem("sums_ready")
        inv_ready = sem("inv_ready")
        diag_ready = sem("diag_ready")
        bc_ready = sem("bc_ready")
        o_ready = sem("o_ready")
        half_ready = sem("half_ready")
        o_summed = sem("o_summed")
        o_scaled = sem("o_scaled")
        o_stored = sem("o_stored")

        wo_loaded = sem("wo_loaded")
        in_loaded = [sem("in_loaded0"), sem("in_loaded1")]
        out_proj = sem("out_proj")
        out_added = sem("out_added")
        out_stored = [sem("out_stored0"), sem("out_stored1")]

        PROJ0, LO0, V0, QKST0, VST0, OADD0, OUT0 = 2 * NM, 8, 4, 32, 16, CT * B, 16

        def wait(eng, s, value):
            if not (isinstance(value, int) and value <= 0):
                eng.wait_ge(s, value)

        def over_heads(eng, head):
            head(0, True, False)
            with eng.Fori(1, NIT - 1) as it:
                head(it, False, False)
            head(NIT - 1, False, True)

        def after(it, g):
            return (it, g + 1) if g + 1 < NG else (it + 1, 0)

        def before(it, g):
            return (it, g - 1) if g > 0 else (it - 1, NG - 1)

        def pair_free(eng, it, g, s):
            it, g, s = (it, g, s - PT) if s >= PT else (*before(it, g), s - PT + NP)
            G = it * NG + g
            if isinstance(G, int) and G < 0:
                return
            eng.wait_ge(pair_used, NP * G + s + 1)
            if s % 2 == 0:
                eng.wait_ge(dve_added, (NP // 2 - 1) * G + max(s // 2, 1))
            else:
                eng.wait_ge(pool_added, (NP // 2 - 1) * G + max(s // 2, 1))

        block = ctx.enter_context(nc.Block())

        @block.sync
        def _(sp):
            sp.dma_start(w_raw, w_qkv[0:128, :]).then_inc(w_loaded, 16)
            for b in range(B):
                for c in range(CT):
                    sp.dma_start(x_sb[:, b * CT + c, :], xT[b, c * 128:(c + 1) * 128, :]).then_inc(
                        x_loaded[b * CT + c], 16)
                    if b == 0 and c > 0:
                        sp.wait_ge(w_hi_done, c)
                        sp.wait_ge(w_lo_done, c)
                        sp.dma_start(w_raw, w_qkv[c * 128:(c + 1) * 128, :]).then_inc(w_loaded, 16)
            sp.dma_start(avg, avg_in).then_inc(consts_loaded, 16)
            sp.dma_start(ident[:], ident_in).then_inc(consts_loaded, 16)

            with sp.Fori(0, NTT) as i:
                for b in range(B):
                    n = 2 * i + b
                    for m in range(8):
                        sp.wait_ge(lo_done, LO0 + 8 * n + m + 1)
                        dram = q_dram if m < 4 else k_dram
                        for hh in range(2):
                            sp.dma_start(
                                dram[b * HEADS + 2 * (m % 4) + hh, :, :, bass.ds(i * TT, TT)].rearrange(
                                    "l d n -> d l n"),
                                qk_stage[hh * D:(hh + 1) * D, m % 4].bitcast(F32),
                            ).then_inc(qk_stored[m % 4], 16)
                    for s in range(4):
                        sp.wait_ge(v_done, V0 + 4 * n + s + 1)
                        sp.dma_start(
                            v_dram[b * HEADS:(b + 1) * HEADS, bass.ds(i * TT + s * 128, 128), :].rearrange(
                                "h t d -> t h d"),
                            v_stage[:, s, :].rearrange("p (h d) -> p h d", h=HEADS),
                        ).then_inc(v_stored[s], 16)

            for s in range(4):
                sp.wait_ge(qk_stored[s], QKST0 + 32 * 2 * B * NTT)
                sp.wait_ge(v_stored[s], VST0 + 16 * B * NTT)
            sp.wait_ge(proj_done, PROJ0 + NM * B * NTT)

            def load_k(tensor, done, it, c):
                sp.dma_start(tensor[:, c * KU:(c + 1) * KU].bitcast(F32),
                             k_dram[it, :, :, c * KU:(c + 1) * KU].rearrange("l d n -> (l d) n")
                             ).then_inc(done[c], 16)

            def load_v(it, c):
                n = NA * 128
                sp.dma_start(v_sb[:, c * NA:(c + 1) * NA, :],
                             v_dram[it, c * n:(c + 1) * n, :].rearrange("(j p) d -> p j d", p=128)
                             ).then_inc(v_in[c], 16)

            def load_q_hi(it, g):
                for half in range(2):
                    sp.dma_start(q_hi[half * D:(half + 1) * D, g % 3].bitcast(F32),
                                 q_dram[it, 0, :, g * GQ:(g + 1) * GQ]).then_inc(q_hi_in[g % 3], 16)

            def load_q_lo(it, g):
                sp.dma_start(q_rows[0:D, g % 2].bitcast(F32),
                             q_dram[it, 1, :, g * GQ:(g + 1) * GQ]).then_inc(q_lo_in[g % 2], 16)

            def copy_k_hi(it, g):
                for qb in range(NQB):
                    sp.dma_start(k_rows[0:D, g % 2, qb].bitcast(F32), k_mov[0:D].bitcast(F32)
                                 ).then_inc(k_rows_in[g % 2], 16)

            def load_bias_tables(it):
                sp.dma_start(row_t[:], row_win[it]).then_inc(bias_in, 16)
                sp.dma_start(col_t[:], col_win[it]).then_inc(bias_in, 16)

            def load_row_tables(it):
                sp.dma_start(rrow_t[:], row_rows[it]).then_inc(rows_in, 16)
                sp.dma_start(rcol_t[:], col_rows[it]).then_inc(rows_in, 16)
                sp.dma_start(rless_t[:], col_less[it]).then_inc(rows_in, 16)

            for par in range(2):
                sp.dma_start(pT[D:128, 0, par, :], onehots).then_inc(onehots_loaded, 16)
            sp.dma_start(neg_lo_t[D:128], neg_lo).then_inc(onehots_loaded, 16)
            load_q_hi(0, 0)
            for c in range(NCB):
                load_k(k_mov, k_mov_in, 0, c)
            load_bias_tables(0)
            load_row_tables(0)
            load_q_lo(0, 0)
            load_q_hi(0, 1)
            for c in range(NCB):
                load_k(k_st, k_st_in, 0, c)
            for c in range(NCB):
                sp.wait_ge(k_mov_in[c], 16)
            copy_k_hi(0, 0)
            for c in range(NCB):
                load_v(0, c)

            def head(it, first, last):
                for g in range(NG):
                    G = it * NG + g
                    wait(sp, pair_filled, NP * G)
                    if g + 1 < NG or not last:
                        load_q_lo(*after(it, g))
                        if g + 1 == NG:
                            for c in range(NCB):
                                sp.wait_ge(k_mov_in[c], 16 * (it + 2))
                        copy_k_hi(*after(it, g))
                    if g + 2 < NG or not last:
                        load_q_hi(*after(*after(it, g)))
                    if g == 1 and not last:
                        sp.wait_ge(rows_summed, ND * (it + 1))
                        load_row_tables(it + 1)
                        sp.wait_ge(bias_ready, NCB * NCB * (it + 1))
                        load_bias_tables(it + 1)
                    if g == NG - 2 and not last:
                        sp.wait_ge(k_rows_in[1], 16 * NQB * NG // 2 * (it + 1))
                        for c in range(NCB):
                            sp.wait_ge(unit_filled, NU * (G + 2) - NCB + c + 1)
                            load_k(k_mov, k_mov_in, it + 1, c)
                    if not (first and g == 0):
                        sp.wait_ge(o_scaled, G)
                        pit, pg = before(it, g)
                        sp.dma_start(o_dram[pit, :, pg * GQ:(pg + 1) * GQ], o_out[:]).then_inc(o_stored, 16)
                    if g == NG - 1 and not last:
                        for c in range(NCB):
                            sp.wait_ge(pair_filled, NP * G + NP // NCB * (c + 1))
                            load_k(k_st, k_st_in, it + 1, c)
                            sp.wait_ge(pair_used, NP * G + NP // NCB * (c + 1))
                            load_v(it + 1, c)

            over_heads(sp, head)
            sp.wait_ge(o_scaled, NIT * NG)
            sp.dma_start(o_dram[NIT - 1, :, (NG - 1) * GQ:], o_out[:]).then_inc(o_stored, 16)

            sp.wait_ge(o_stored, 16 * NIT * NG)
            sp.dma_start(wo_sb[:], w_out.rearrange("(c p) n -> p c n", p=128)).then_inc(wo_loaded, 16)

            def load_tile(i, b):
                tok = bass.ds(i * TT, TT)
                for c in range(CT):
                    sp.dma_start(o_in[:, b, c, :], o_dram[b * HEADS + 2 * c:b * HEADS + 2 * c + 2, :, tok]
                                 .rearrange("h d n -> (h d) n")).then_inc(in_loaded[b], 16)
                sp.dma_start(x_in[:, b], xT[b, :, tok].rearrange("(c p) n -> p c n", p=128)).then_inc(
                    in_loaded[b], 16)

            load_tile(0, 0)
            load_tile(0, 1)

            def tile_out(i, last):
                for b in range(B):
                    sp.wait_ge(out_added, OADD0 + CT * (B * i + b + 1))
                    sp.dma_start(outT[b, :, bass.ds(i * TT, TT)].rearrange("(c p) n -> p c n", p=128),
                                 y_out[:, b]).then_inc(out_stored[b], 16)
                    if not last:
                        load_tile(i + 1, b)

            with sp.Fori(0, NTT - 1) as i:
                tile_out(i, False)
            tile_out(NTT - 1, True)
            for b in range(B):
                sp.wait_ge(out_stored[b], OUT0 + 16 * NTT)

        @block.tensor
        def _(pe):
            pe.wait_ge(consts_loaded, 32)
            for k in range(2):
                pe.wait_ge(stats_step, k + 1)
                nc.tensor.matmul(ps[:, 0, 0:B * CT], avg, stat[:, k, :], start=True, stop=True).then_inc(
                    group_avg, 1)

            pe.wait_ge(w_hi_done, CT)
            pe.wait_ge(w_lo_done, CT)
            pe.wait_ge(stats_step, 3)
            with pe.Fori(0, NTT) as i:
                for b in range(B):
                    n = 2 * i + b
                    pe.wait_ge(x_lo_done, n + 1)
                    for m in range(NM):
                        was = m - 8 if m >= 8 else m + 4
                        of = n if m >= 8 else n - 1
                        if was < 8:
                            pe.wait_ge(lo_done, LO0 + 8 * of + was + 1)
                        else:
                            pe.wait_ge(v_done, V0 + 4 * of + was - 8 + 1)
                        bank = ps[:, (b * NM + m) % 8, :]
                        steps = [(w, x, c) for c in range(CT)
                                 for w, x in ((w_hi, x_hi), (w_hi, x_lo), (w_lo, x_hi))]
                        for k, (w, x, c) in enumerate(steps):
                            if m < 8:
                                lhs, rhs = w[:, c, m * 128:(m + 1) * 128], x[:, b, c, :]
                            else:
                                lhs, rhs = x[:, b, c, (m - 8) * 128:(m - 7) * 128], w[:, c, 2 * C:3 * C]
                            mm = nc.tensor.matmul(bank, lhs, rhs, start=(k == 0), stop=(k == len(steps) - 1))
                        mm.then_inc(proj_done, 1)

            pe.wait_ge(lo_done, LO0 + 8 * B * NTT)
            pe.wait_ge(v_done, V0 + 4 * B * NTT)
            pe.wait_ge(ones_set, 1)

            def drained(it, g, fill, has_units):
                back, (kind, n) = user_before(FILLS.index(fill), lambda f: f[0] == "S" or has_units)
                G = it * NG + g - back
                if kind == "M":
                    wait(pe, unit_maxed, NU * (G + 1) + n + 1)
                else:
                    wait(pe, exp_done, NP * G + n + 1)

            def max_unit(it, g, u, slot):
                t, c = u // NCB, u % NCB
                if u == 0:
                    pe.wait_ge(q_hi_in[g % 3], 32 * (NG // 3 * it + g // 3 + 1))
                if g == 0 and t == 0:
                    pe.wait_ge(k_mov_in[c], 16 * (it + 1))
                for half in range(2):
                    mm = nc.tensor.matmul(
                        ps_slot[slot][:, half, :], q_hi[:, g % 3, t * 128:(t + 1) * 128],
                        k_mov[:, c * KU + half * 512:c * KU + (half + 1) * 512], start=True, stop=True)
                mm.then_inc(unit_filled, 1)

            def max_rows(it, g):
                pe.wait_ge(max_ready, GT * (it * NG + g + 1))
                for t in range(GT):
                    mm = nc.tensor.matmul(
                        ps_x[:, t * 128:(t + 1) * 128],
                        neg_max[:, g % 2, t:t + 1].to_broadcast([128, 128]), ident_r[:],
                        start=True, stop=True)
                mm.then_inc(max_row, 1)

            def score_pair(it, g, s, slot):
                G = it * NG + g
                if s == 0:
                    pe.wait_ge(q_lo_in[g % 2], 16 * (NG // 2 * it + g // 2 + 1))
                    pe.wait_ge(max_row_set, G + 1)
                    pe.wait_ge(k_rows_in[g % 2], 16 * NQB * (NG // 2 * it + g // 2 + 1))
                    pe.wait_ge(k_rows_set, NQB * NCB * (G + 1))
                if g == 0 and s % (NP // NCB) == 0:
                    pe.wait_ge(k_st_in[s // (NP // NCB)], 16 * (it + 1))
                for h in range(2):
                    j = 2 * s + h
                    bank = ps_slot[slot][:, h, :]
                    for qb in range(NQB):
                        n = GQ // NQB
                        nc.tensor.matmul(
                            bank[:, qb * n:(qb + 1) * n], k_rows[0:KB, g % 2, qb, j * 128:(j + 1) * 128],
                            q_rows[0:KB, g % 2, qb * n:(qb + 1) * n], start=(qb == 0), stop=False,
                            skip_group_check=True)
                    mm = nc.tensor.matmul(bank, k_st[:, j * 128:(j + 1) * 128], q_hi[:, g % 3, :],
                                          start=False, stop=True, skip_group_check=True)
                mm.then_inc(pair_filled, 1)

            def products(it, g, s):
                G = it * NG + g
                if s == 0:
                    wait(pe, o_summed, G)
                if g == 0 and s % (NP // NCB) == 0:
                    pe.wait_ge(v_in[s // (NP // NCB)], 16 * (it + 1))
                pe.wait_ge(exp_done, NP * G + s + 1)
                for h in range(2):
                    mm = nc.tensor.matmul(ps_o[h * D:(h + 1) * D, :], v_sb[:, 2 * s + h, :],
                                          pT[:, s % PT, h, :], start=(s == 0), stop=(s == NP - 1))
                mm.then_inc(pair_used, 1)

            def row_sums(it, g):
                pe.wait_ge(acc_ready, it * NG + g + 1)
                for t in range(GT):
                    mm = nc.tensor.matmul(ps_x[:, t:t + 1], acc[:, t * 128:(t + 1) * 128], ones[:, 0:1],
                                          start=True, stop=True)
                mm.then_inc(sums_ready, 1)

            def broadcast(it, g):
                pe.wait_ge(diag_ready, it * NG + g + 1)
                nc.tensor.matmul(ps_x[0:D, :], ones[:], diag.rearrange("p t n -> p (t n)"),
                                 start=True, stop=True).then_inc(bc_ready, 1)

            for u in range(NU):
                wait(pe, unit_maxed, u - NSLOT + 1)
                max_unit(0, 0, u, u % NSLOT)
            pe.wait_ge(onehots_set, 2)
            max_rows(0, 0)
            pe.wait_ge(unit_maxed, NU)

            def head(it, first, last):
                for g in range(NG):
                    has_units = not (last and g == NG - 1)
                    for s in range(NP):
                        if s == NP - 1 and has_units:
                            if not (first and g == 0):
                                pe.wait_ge(o_scaled, it * NG + g)
                            else:
                                pe.wait_ge(max_row_set, 1)
                            max_rows(*after(it, g))
                        for kind, n in FILLS:
                            if kind == "S" and n == s:
                                drained(it, g, (kind, n), has_units)
                                score_pair(it, g, n, FILLS.index((kind, n)) % NSLOT)
                            elif kind == "M" and UNIT_STEP[n] == s and has_units:
                                drained(it, g, (kind, n), has_units)
                                max_unit(*after(it, g), n, FILLS.index((kind, n)) % NSLOT)
                        if s == 2:
                            products(it, g, 0)
                        if s > 1:
                            products(it, g, s - 1)
                        if s == 0 and not (first and g == 0):
                            products(*before(it, g), NP - 1)
                        if not (first and g == 0):
                            if s == SUM_STEP:
                                row_sums(*before(it, g))
                            if s == BC_STEP:
                                broadcast(*before(it, g))

            over_heads(pe, head)
            products(NIT - 1, NG - 1, NP - 1)
            row_sums(NIT - 1, NG - 1)
            broadcast(NIT - 1, NG - 1)

            pe.wait_ge(wo_loaded, 16)
            pe.wait_ge(o_scaled, NIT * NG)
            with pe.Fori(0, NTT) as i:
                for b in range(B):
                    pe.wait_ge(in_loaded[b], 16 * (CT + 1) * (i + 1))
                    pe.wait_ge(out_added, OADD0 + CT * (B * (i - 1) + b + 1))
                    for m in range(CT):
                        for c in range(CT):
                            mm = nc.tensor.matmul(ps[:, b * CT + m, :], wo_sb[:, c, m * 128:(m + 1) * 128],
                                                  o_in[:, b, c, :], start=(c == 0), stop=(c == CT - 1))
                        mm.then_inc(out_proj, 1)

        @block.scalar
        def _(act):
            for c in range(CT):
                act.wait_ge(w_loaded, 16 * (c + 1))
                nc.scalar.activation(w_hi[:, c, :], w_raw, ACT.Copy).then_inc(w_hi_done, 1)
            act.wait_ge(stats_step, 3)
            nc.scalar.activation(stat[:, 3, :], stat[:, 2, :], ACT.Sqrt).then_inc(root_done, 1)

            def split_x(i, b):
                act.wait_ge(x_normed, 2 * i + b + 1)
                nc.scalar.activation(x_hi[:, b], x_sb[:, b * CT:(b + 1) * CT, bass.ds(i * TT, TT)],
                                     ACT.Copy).then_inc(x_hi_done, 1)

            def evacuate(i, b):
                n = 2 * i + b
                for m in range(NM):
                    act.wait_ge(proj_done, PROJ0 + NM * n + m + 1)
                    bank = ps[:, (b * NM + m) % 8, :]
                    if m < 8:
                        act.wait_ge(qk_stored[m % 4], QKST0 + 32 * (2 * n + m // 4))
                        nc.scalar.activation(qk_stage[:, m % 4, 0, :], bank, ACT.Copy,
                                             scale=SCALE if m < 4 else 1.0).then_inc(hi_done, 1)
                    else:
                        act.wait_ge(v_stored[m - 8], VST0 + 16 * n)
                        nc.scalar.activation(v_stage[:, m - 8, :], bank, ACT.Copy).then_inc(v_done, 1)

            split_x(0, 0)
            with act.Fori(0, NTT - 1) as i:
                split_x(i, 1)
                evacuate(i, 0)
                split_x(i + 1, 0)
                evacuate(i, 1)
            split_x(NTT - 1, 1)
            evacuate(NTT - 1, 0)
            evacuate(NTT - 1, 1)

            act.wait_ge(proj_done, PROJ0 + NM * B * NTT)
            for s in range(4):
                act.wait_ge(qk_stored[s], QKST0 + 32 * 2 * B * NTT)
                act.wait_ge(v_stored[s], VST0 + 16 * B * NTT)
            act.wait_ge(onehots_loaded, 48)
            nc.scalar.activation(q_rows[D:128], pT[D:128, 0], ACT.Copy).then_inc(onehots_set, 1)
            act.wait_ge(consts_loaded, 32)
            nc.scalar.activation(ident_r[:], ident[:], ACT.Copy).then_inc(onehots_set, 1)

            def copy_rows(it, g, k):
                qb, c = k // NCB, k % NCB
                first_row = IMG_H - QB - QB * (NQB * (g % 2) + qb)
                nc.scalar.activation(
                    k_rows[D:128, g % 2, qb, c * KU:(c + 1) * KU],
                    rows[D:128, c - g // 2 + NCB - 1, first_row * CB:first_row * CB + KU].bitcast(F32),
                    ACT.Copy).then_inc(k_rows_set, 1)

            def set_max_row(it, g):
                act.wait_ge(max_row, it * NG + g + 1)
                nc.scalar.activation(q_rows[D:D + 1, g % 2, :], ps_x[0:1, :], ACT.Copy).then_inc(max_row_set, 1)

            def exp(it, g, s):
                G = it * NG + g
                pair_free(act, it, g, s)
                act.wait_ge(pair_filled, NP * G + s + 1)
                slot = FILLS.index(("S", s)) % NSLOT
                nc.scalar.activation(pT[:, s % PT], ps_slot[slot], ACT.Exp).then_inc(exp_done, 1)

            def half(it, g):
                act.wait_ge(pair_used, NP * (it * NG + g + 1))
                wait(act, o_scaled, it * NG + g)
                nc.scalar.activation(o_sum[:], ps_o[D:2 * D, :], ACT.Copy).then_inc(half_ready, 1)

            def round_rows(n, d):
                act.wait_ge(rows_summed, n + 1)
                nc.scalar.activation(rows[D:128, d, :], rows_sum[D:128], ACT.Copy).then_inc(rows_rounded, 1)

            for n, d in enumerate(FIRST_ROWS):
                round_rows(n, d)
            act.wait_ge(rows_ready, 2 * len(FIRST_ROWS))
            for k in range(NQB * NCB):
                copy_rows(0, 0, k)
            set_max_row(0, 0)

            def head(it, first, last):
                for g in range(NG):
                    for s in range(NP):
                        if s == HALF_STEP and not (first and g == 0):
                            half(*before(it, g))
                        if s == NP - 1 and not (last and g == NG - 1):
                            set_max_row(*after(it, g))
                        exp(it, g, s)
                        if s in TABLE_STEPS and not (last and g == NG - 1):
                            nit, ng = after(it, g)
                            if s == TABLE_STEPS[0] and ng % 2 == 0:
                                built = len(FIRST_ROWS) + ND * it + {0: 4, 2: 0, 4: 1}[ng]
                                act.wait_ge(rows_ready, 2 * built)
                            copy_rows(nit, ng, TABLE_STEPS.index(s))
                        for k, (bg, d, nxt) in enumerate(ROW_BUILDS):
                            if (bg, HI_STEP) == (g, s) and not (nxt and last):
                                act.wait_ge(k_rows_set, NQB * NCB * (it * NG + g + 2))
                                round_rows(len(FIRST_ROWS) + ND * it + k, d)

            over_heads(act, head)
            half(NIT - 1, NG - 1)

        @block.gpsimd
        def _(pool):
            pool.wait_ge(proj_done, PROJ0 + NM * B * NTT)
            for s in range(4):
                pool.wait_ge(qk_stored[s], QKST0 + 32 * 2 * B * NTT)
                pool.wait_ge(v_stored[s], VST0 + 16 * B * NTT)
            nc.gpsimd.memset(ones[:], 1.0).then_inc(ones_set, 1)
            group_reg = pool.alloc_register("groups")
            pool.reg_mov(group_reg, 0)

            def build_bias(it, cb, kb):
                pool.wait_ge(bias_in, 32 * (it + 1))
                nc.gpsimd.tensor_tensor(
                    bias[:, cb, kb, :].rearrange("p (u j) -> p u j", j=CB),
                    row_t[:].unsqueeze(2).to_broadcast([128, UR, CB]),
                    col_t[:, cb, kb, :].unsqueeze(1).to_broadcast([128, UR, CB]), ALU.add
                ).then_inc(bias_ready, 1)

            def sum_rows(n, d):
                wait(pool, rows_ready, 2 * n)
                nc.gpsimd.tensor_tensor(
                    rows_sum[:].rearrange("p (u j) -> p u j", j=CB),
                    rrow_t[:].unsqueeze(2).to_broadcast([128, WR, CB]),
                    rcol_t[:, d, :].unsqueeze(1).to_broadcast([128, WR, CB]), ALU.add
                ).then_inc(rows_summed, 1)

            def subtract_columns(it):
                pool.wait_ge(rows_in, 48 * (it + 1))
                nc.gpsimd.tensor_tensor(rcol_t[:], rcol_t[:], rless_t[:], ALU.subtract
                                        ).then_inc(cols_less, 1)
                pool.wait_ge(cols_less, it + 1)

            def add_pair(it, g, s):
                G = it * NG + g
                n = (NP // 2 - 1) * G + s // 2
                if s == 3:
                    wait(pool, acc_merged, G)
                pool.wait_ge(exp_done, NP * G + s + 1)
                if s == 3:
                    src = pT[:, 1 % PT]
                else:
                    pool.wait_ge(pool_added, n - 1)
                    src = acc_p[:]
                nc.gpsimd.tensor_tensor(acc_p[:], src, pT[:, s % PT], ALU.add).then_inc(pool_added, 1)

            def diagonals(it, g):
                pool.reg_add(group_reg, group_reg, 1)
                pool.wait_ge(consts_loaded, 32)
                pool.wait_ge(inv_ready, group_reg)
                for t in range(GT):
                    op = nc.gpsimd.tensor_scalar(diag[:, t, :], ident[:], inv_t[:, t:t + 1], None, ALU.mult)
                op.then_inc(diag_ready, 1)

            subtract_columns(0)
            for n, d in enumerate(FIRST_ROWS):
                sum_rows(n, d)
            for cb in range(2):
                for kb in range(NCB):
                    build_bias(0, cb, kb)

            def head(it, first, last):
                for g in range(NG):
                    G = it * NG + g
                    for s in range(NP):
                        if s == 0 and not (first and g == 0):
                            add_pair(*before(it, g), NP - 1)
                        if s >= 4 and s % 2 == 0:
                            add_pair(it, g, s - 1)
                        if s == DIAG_STEP and not (first and g == 0):
                            diagonals(*before(it, g))
                        what = BUILDS.get((g, s))
                        if what is None or (what[-1] and last):
                            continue
                        if what[0] == "E":
                            wait(pool, unit_maxed, NU * (G + 1))
                            build_bias(it + what[-1], what[1], what[2])
                        else:
                            k = ROW_BUILDS.index((g, *what[1:]))
                            if k == 1:
                                subtract_columns(it + 1)
                            sum_rows(len(FIRST_ROWS) + ND * it + k, what[1])

            over_heads(pool, head)
            add_pair(NIT - 1, NG - 1, NP - 1)
            diagonals(NIT - 1, NG - 1)

        @block.vector
        def _(dve):
            unit_reg = dve.alloc_register("units")
            dve.reg_mov(unit_reg, 0)
            for s, value in ((proj_done, PROJ0), (lo_done, LO0), (v_done, V0), (out_added, OADD0),
                             *((q, QKST0) for q in qk_stored), *((q, VST0) for q in v_stored),
                             *((q, OUT0) for q in out_stored)):
                dve.sem_inc(s, value)

            own_n = 0

            def own(op):
                nonlocal own_n
                own_n += 1
                op.then_inc(stats_own, 1)
                dve.wait_ge(stats_own, own_n)

            for i in range(B * CT):
                if i < CT:
                    dve.wait_ge(w_hi_done, i + 1)
                    nc.vector.tensor_tensor(w_lo[:, i, :], w_raw, w_hi[:, i, :].bitcast(F32), ALU.subtract
                                            ).then_inc(w_lo_done, 1)
                dve.wait_ge(x_loaded[i], 16)
                for k in range(NTT):
                    op = nc.vector.bn_stats(bn[:, k, :], x_sb[:, i, k * TT:(k + 1) * TT])
                own(op)
                own(nc.vector.bn_aggr(mv[:, i, :], bn))
            V = nc.vector
            V.tensor_copy(stat[:, 0, :], mv[:, :, 0]).then_inc(stats_step, 1)
            dve.wait_ge(group_avg, 1)
            own(V.tensor_copy(stat[:, 4, :], ps[:, 0, 0:B * CT]))
            own(V.tensor_tensor(stat[:, 5, :], stat[:, 0, :], stat[:, 4, :], ALU.subtract))
            own(V.tensor_tensor(stat[:, 6, :], stat[:, 5, :], stat[:, 5, :], ALU.mult))
            V.tensor_tensor(stat[:, 1, :], stat[:, 6, :], mv[:, :, 1], ALU.add).then_inc(stats_step, 1)
            dve.wait_ge(group_avg, 2)
            V.tensor_scalar(stat[:, 2, :], ps[:, 0, 0:B * CT], EPS, None, ALU.add).then_inc(stats_step, 1)
            dve.wait_ge(root_done, 1)
            own(V.reciprocal(stat[:, 5, :], stat[:, 3, :]))
            own(V.tensor_tensor(stat[:, 6, :], stat[:, 2, :], stat[:, 5, :], ALU.mult))
            own(V.tensor_tensor(stat[:, 7, :], stat[:, 6, :], stat[:, 3, :], ALU.add))
            own(V.tensor_scalar(stat[:, 5, :], stat[:, 7, :], 0.5, None, ALU.mult))
            own(V.reciprocal(stat[:, 8, :], stat[:, 5, :]))

            def normalised(i, b):
                dve.wait_ge(proj_done, PROJ0 + NM * (2 * i + b - 1))
                for c in range(CT):
                    k = b * CT + c
                    x = x_sb[:, k, bass.ds(i * TT, TT)]
                    op = nc.vector.tensor_scalar(x, x, stat[:, 4, k:k + 1], stat[:, 8, k:k + 1],
                                                 ALU.subtract, ALU.mult)
                op.then_inc(x_normed, 1)

            def low_x(i, b):
                dve.wait_ge(x_hi_done, 2 * i + b + 1)
                nc.vector.tensor_tensor(x_lo[:, b], x_sb[:, b * CT:(b + 1) * CT, bass.ds(i * TT, TT)],
                                        x_hi[:, b].bitcast(F32), ALU.subtract).then_inc(x_lo_done, 1)

            def low_qk(i, b):
                n = 2 * i + b
                for m in range(8):
                    dve.wait_ge(hi_done, 8 * n + m + 1)
                    stage = qk_stage[:, m % 4]
                    nc.vector.scalar_tensor_tensor(
                        out=stage[:, 1, :], in0=ps[:, (b * NM + m) % 8, :], scalar=SCALE if m < 4 else 1.0,
                        in1=stage[:, 0, :].bitcast(F32), op0=ALU.mult, op1=ALU.subtract).then_inc(lo_done, 1)

            normalised(0, 0)
            low_x(0, 0)
            with dve.Fori(0, NTT - 1) as i:
                normalised(i, 1)
                low_x(i, 1)
                low_qk(i, 0)
                normalised(i + 1, 0)
                low_x(i + 1, 0)
                low_qk(i, 1)
            normalised(NTT - 1, 1)
            low_x(NTT - 1, 1)
            low_qk(NTT - 1, 0)
            low_qk(NTT - 1, 1)

            dve.wait_ge(proj_done, PROJ0 + NM * B * NTT)
            for s in range(4):
                dve.wait_ge(qk_stored[s], QKST0 + 32 * 2 * B * NTT)
                dve.wait_ge(v_stored[s], VST0 + 16 * B * NTT)
            dve.wait_ge(onehots_loaded, 48)

            def low_rows(n, d, part):
                dve.wait_ge(rows_rounded, n + 1)
                at = slice(part * WR // 2 * CB, (part + 1) * WR // 2 * CB)
                r = rows[D:128, d, at]
                nc.vector.scalar_tensor_tensor(
                    out=r, in0=r.bitcast(F32), scalar=neg_lo_t[D:128], in1=rows_sum[D:128, at],
                    op0=ALU.mult, op1=ALU.add).then_inc(rows_ready, 1)

            def max_unit(it, g, u):
                G, t, c = it * NG + g, u // NCB, u % NCB
                U = NU * G + u
                tile = g * GT + t
                cb, a = tile // NA, tile % NA
                if g % 2 == 0 and u == 0:
                    dve.wait_ge(bias_ready, NCB * (NCB * it + cb + 1))
                dve.reg_add(unit_reg, unit_reg, 1)
                dve.wait_ge(stats_step, 3)
                dve.wait_ge(unit_filled, unit_reg)
                row = (IMG_H - TR - TR * a) * CB
                slot = u % NSLOT if isinstance(U, int) and U < NU else FILLS.index(("M", u)) % NSLOT
                nc.vector.tensor_tensor_reduce(
                    out=junk[:, c, :], in0=ps_slot[slot].rearrange("p a n -> p (a n)"),
                    in1=bias[:, cb, c, row:row + KU], scale=1.0, scalar=LOWEST,
                    op0=ALU.add, op1=ALU.max, accum_out=maxes[:, g % 2, t, c:c + 1]).then_inc(unit_maxed, 1)
                if c == NCB - 1:
                    dve.wait_ge(unit_maxed, U + 1)
                    nc.vector.tensor_reduce(neg_max[:, g % 2, t:t + 1], maxes[:, g % 2, t, :], AX_X, ALU.max,
                                            negate=True).then_inc(max_ready, 1)

            def add_pair(it, g, s):
                G = it * NG + g
                n = (NP // 2 - 1) * G + s // 2
                dve.wait_ge(exp_done, NP * G + s + 1)
                if s == 2:
                    wait(dve, acc_ready, G)
                    src = pT[:, 0]
                else:
                    dve.wait_ge(dve_added, n - 1)
                    src = acc_d[:]
                nc.vector.tensor_tensor(acc_d[:], src, pT[:, s % PT], ALU.add).then_inc(dve_added, 1)

            def merge(it, g):
                G = it * NG + g
                dve.wait_ge(pool_added, (NP // 2 - 1) * (G + 1))
                dve.wait_ge(dve_added, (NP // 2 - 1) * (G + 1))
                nc.vector.tensor_tensor(acc_d[:], acc_d[:], acc_p[:], ALU.add).then_inc(acc_merged, 1)
                dve.wait_ge(acc_merged, G + 1)
                nc.vector.tensor_tensor(acc[:], acc_d[:, 0, :], acc_d[:, 1, :], ALU.add).then_inc(acc_ready, 1)

            def inverse(it, g):
                dve.wait_ge(sums_ready, it * NG + g + 1)
                nc.vector.reciprocal(inv_t[:], ps_x[:, 0:GT]).then_inc(inv_ready, 1)

            def add_half(it, g):
                G = it * NG + g
                dve.wait_ge(half_ready, G + 1)
                nc.vector.tensor_tensor(o_sum[:], ps_o[0:D, :], o_sum[:], ALU.add).then_inc(o_summed, 1)

            def output(it, g):
                G = it * NG + g
                dve.wait_ge(bc_ready, G + 1)
                wait(dve, o_stored, 16 * G)
                dve.wait_ge(o_summed, G + 1)
                nc.vector.tensor_tensor(o_out[:], ps_x[0:D, :], o_sum[:], ALU.mult).then_inc(o_scaled, 1)

            for n, d in enumerate(FIRST_ROWS):
                low_rows(n, d, 0)
                low_rows(n, d, 1)
            for u in range(NU):
                max_unit(0, 0, u)

            def head(it, first, last):
                for g in range(NG):
                    for s in range(NP):
                        if not (first and g == 0):
                            if s == ADD_STEP:
                                add_half(*before(it, g))
                            if s == MERGE_STEP:
                                merge(*before(it, g))
                            if s == INV_STEP:
                                inverse(*before(it, g))
                            if s == OUT_STEP:
                                output(*before(it, g))
                        if s >= 3 and s % 2 == 1:
                            add_pair(it, g, s - 1)
                        if not (last and g == NG - 1):
                            for u in range(NU):
                                if UNIT_STEP[u] == s:
                                    max_unit(*after(it, g), u)
                        for k, (bg, d, nxt) in enumerate(ROW_BUILDS):
                            if bg == g and s in LO_STEPS and not (nxt and last):
                                low_rows(len(FIRST_ROWS) + ND * it + k, d, LO_STEPS.index(s))

            over_heads(dve, head)
            add_half(NIT - 1, NG - 1)
            merge(NIT - 1, NG - 1)
            inverse(NIT - 1, NG - 1)
            output(NIT - 1, NG - 1)

            with dve.Fori(0, NTT) as i:
                for b in range(B):
                    dve.wait_ge(out_stored[b], OUT0 + 16 * i)
                    dve.wait_ge(in_loaded[b], 16 * (CT + 1) * (i + 1))
                    for m in range(CT):
                        dve.wait_ge(out_proj, CT * (B * i + b) + m + 1)
                        nc.vector.tensor_tensor(y_out[:, b, m, :], ps[:, b * CT + m, :], x_in[:, b, m, :],
                                                ALU.add).then_inc(out_added, 1)


def kernel(x, L0_conv_w_qkv, L0_conv_w_out, L0_conv_rel_row_tab, L0_conv_rel_col_tab):
    from concourse import bacc
    from concourse.bass_utils import run_bass_kernel_spmd

    row_tab, col_tab = np.asarray(L0_conv_rel_row_tab), np.asarray(L0_conv_rel_col_tab)
    xT = np.asarray(x).reshape(B, IMG_H, NCB, CB, C).transpose(0, 4, 2, 1, 3).reshape(B, C, S)
    p = np.arange(128)
    row_at = (p // CB)[:, None] - np.arange(UR)[None, :] + (IMG_H - TR) + IMG_H - 1
    blocks = np.arange(NCB) * CB
    col = np.arange(CB)
    col_at = ((p % CB)[:, None, None, None] + blocks[None, :, None, None] - blocks[None, None, :, None]
              - col[None, None, None, :] + IMG_W - 1)
    r_at = np.arange(QB)[:, None] - np.arange(WR)[None, :] + (IMG_H - QB) + IMG_H - 1
    c_at = (col[:, None, None] - (np.arange(ND) - (NCB - 1))[None, :, None] * CB - col[None, None, :]
            + IMG_W - 1)
    R, Cc = row_tab.T[:, r_at], col_tab.T[:, c_at]
    row_rows = np.zeros((HEADS, 128, WR), row_tab.dtype)
    col_rows = np.zeros((HEADS, 128, ND, CB), col_tab.dtype)
    col_less = np.zeros((HEADS, 128, ND, CB), col_tab.dtype)
    neg_lo = np.zeros((64, 1), np.float32)
    hots = np.zeros((64, GQ), np.float32)
    col_rows[:, D] = 1
    q = np.arange(GQ)
    q_row, q_col = q // CB % QB, q % CB
    for part in range(2):
        r0, c0 = 1 + part * QB, 1 + 2 * QB + part * (CB - 1)
        row_rows[:, D + r0:D + r0 + QB] = R
        col_rows[:, D + r0:D + r0 + QB] = Cc[:, 0:1]
        col_rows[:, D + c0:D + c0 + CB - 1] = Cc[:, 1:]
        col_less[:, D + c0:D + c0 + CB - 1] = Cc[:, 0:1]
        hots[r0:r0 + QB] = q_row == np.arange(QB)[:, None]
        hots[c0:c0 + CB - 1] = q_col == np.arange(1, CB)[:, None]
        if part == 1:
            neg_lo[r0:r0 + QB] = -1
            neg_lo[c0:c0 + CB - 1] = -1
    group = np.arange(128) // NORM_G
    arrays = {
        "xT": xT, "w_qkv": np.asarray(L0_conv_w_qkv), "w_out": np.asarray(L0_conv_w_out),
        "row_win": np.tile(row_tab.T[:, row_at], (B, 1, 1)),
        "col_win": np.tile(col_tab.T[:, col_at], (B, 1, 1, 1, 1)),
        "row_rows": np.tile(row_rows, (B, 1, 1)), "col_rows": np.tile(col_rows, (B, 1, 1, 1)),
        "col_less": np.tile(col_less, (B, 1, 1, 1)), "neg_lo": neg_lo, "onehots": hots,
        "ident": np.eye(128, dtype=np.float32),
        "avg": ((group[:, None] == group[None, :]) / NORM_G).astype(np.float32),
    }
    arrays = {f"in_{k}": np.ascontiguousarray(v) for k, v in arrays.items()}
    nc = bacc.Bacc("TRN2", target_bir_lowering=False, num_devices=1)
    aps = [nc.dram_tensor(k, v.shape, mybir.dt.from_np(v.dtype), kind="ExternalInput").ap()
           for k, v in arrays.items()]
    out = nc.dram_tensor("outT", (B, C, S), F32, kind="ExternalOutput").ap()
    attention_kernel(nc, *aps, out)
    result = run_bass_kernel_spmd(nc, [arrays], core_ids=[0]).results[0]["outT"]
    return np.ascontiguousarray(
        result.reshape(B, C, NCB, IMG_H, CB).transpose(0, 3, 2, 4, 1).reshape(B, IMG_H, IMG_W, C))
```

```python
from contextlib import ExitStack

import concourse.bass as bass
import numpy as np
from concourse import mybir

F32 = mybir.dt.float32
F32R = mybir.dt.float32r
BF16 = mybir.dt.bfloat16
ALU = mybir.AluOpType
ACT = mybir.ActivationFunctionType
AX_X = mybir.AxisListType.X

B, IMG_H, IMG_W, C = 2, 64, 48, 512
HEADS, D = 8, 64
S = IMG_H * IMG_W
NIT = B * HEADS
CB = 16
NCB = IMG_W // CB
TR = 128 // CB
NA = IMG_H // TR
KU = S // NCB
GT = 4
GQ = GT * 128
NG = S // GQ
NU = GT * NCB
NP = S // 256
UR = 2 * IMG_H - TR
QB = 16
NQB = GQ // (QB * CB)
WR = 2 * IMG_H - QB
ND = 2 * NCB - 1
MROWS = 1 + 2 * (QB + CB - 1)
KB = D + MROWS
CT = C // 128
TT = 512
NTT = S // TT
NORM_G = 16
EPS = 1e-5
SCALE = D ** -0.5
LOWEST = float(np.finfo(np.float32).min)
NM = 12

UNIT_STEP = [0, 1, 1, 3, 3, 4, 5, 6, 6, 8, 8, 9]
PT = 4
FILLS = [f for s in range(NP) for f in [("S", s)] + [("M", u) for u in range(NU) if UNIT_STEP[u] == s]]
NSLOT = 3
assert len(FILLS) % NSLOT == 0 and NU % NSLOT == 0
HALF_STEP, ADD_STEP, MERGE_STEP, SUM_STEP, INV_STEP, DIAG_STEP, BC_STEP, OUT_STEP = 1, 1, 2, 3, 4, 5, 6, 7
TABLE_STEPS = [3, 4, 5, 6, 7, 8]
BUILDS = {
    (0, 1): ("E", 2, 0, 0), (0, 6): ("R", 0, 0), (0, 8): ("E", 2, 1, 0),
    (1, 1): ("E", 2, 2, 0),
    (2, 1): ("E", 0, 0, 1), (2, 6): ("R", 4, 1), (2, 8): ("E", 0, 1, 1),
    (3, 1): ("E", 0, 2, 1), (3, 6): ("R", 3, 1), (3, 8): ("E", 1, 0, 1),
    (4, 1): ("E", 1, 1, 1), (4, 6): ("R", 2, 1),
    (5, 1): ("E", 1, 2, 1), (5, 6): ("R", 1, 1),
}
ROW_BUILDS = [(g, what[1], what[2]) for (g, s), what in BUILDS.items() if what[0] == "R"]
HI_STEP, LO_STEPS = 9, (10, 11)
FIRST_ROWS = (2, 3, 4, 1)


def user_before(k, present):
    back, k = 0, k - NSLOT
    while True:
        if k < 0:
            back, k = back + 1, k + len(FILLS)
        if back or present(FILLS[k]):
            return back, FILLS[k]
        k -= NSLOT


def attention_kernel(nc, xT, w_qkv, w_out, row_win, col_win, row_rows, col_rows, col_less, neg_lo,
                     onehots, ident_in, avg_in, outT):
    with ExitStack() as ctx:
        def sb(name, shape, dt=F32, stack=ctx):
            return stack.enter_context(nc.sbuf_tensor(name, shape, dt))

        def sem(name):
            return ctx.enter_context(nc.semaphore(name))

        q_dram = nc.dram_tensor("q_scratch", [NIT, 2, D, S], F32).ap()
        k_dram = nc.dram_tensor("k_scratch", [NIT, 2, D, S], F32).ap()
        v_dram = nc.dram_tensor("v_scratch", [NIT, S, D], F32).ap()
        o_dram = nc.dram_tensor("o_scratch", [NIT, D, S], F32).ap()

        ident = sb("ident", [128, 128])

        with ExitStack() as one:
            x_sb = sb("x_sb", [128, B * CT, S], F32, one)
            w_hi = sb("w_hi", [128, CT, 3 * C], F32R, one)
            w_lo = sb("w_lo", [128, CT, 3 * C], F32R, one)
            x_hi = sb("x_hi", [128, 2, CT, TT], F32R, one)
            x_lo = sb("x_lo", [128, 2, CT, TT], F32R, one)
            qk_stage = sb("qk_stage", [128, 4, 2, TT], F32R, one)
            v_stage = sb("v_stage", [128, 4, TT], F32, one)
            small = sb("small", [128, 336], F32, one)
            avg = small[:, 0:128]
            bn = small[:, 128:128 + NTT * 6].rearrange("p (k s) -> p k s", s=6)
            mv = small[:, 192:192 + B * CT * 2].rearrange("p (i s) -> p i s", s=2)
            stat = small[:, 256:256 + 9 * B * CT].rearrange("p (s i) -> p s i", i=B * CT)
        w_raw = v_stage.rearrange("p a n -> p (a n)")[:, 0:3 * C]
        with ExitStack() as two:
            bias = sb("bias", [128, NCB, NCB, UR * CB], BF16, two)
            rows = sb("rows", [128, ND, WR * CB], F32R, two)
            rows_sum = sb("rows_sum", [128, WR * CB], F32, two)
            k_mov = sb("k_mov", [128, S], F32R, two)
            k_st = sb("k_st", [128, S], F32R, two)
            k_rows = sb("k_rows", [128, 2, NQB, S], F32R, two)
            q_hi = sb("q_hi", [128, 3, GQ], F32R, two)
            q_rows = sb("q_rows", [128, 2, GQ], F32R, two)
            v_sb = sb("v_sb", [128, S // 128, D], F32, two)
            pT = sb("pT", [128, PT, 2, GQ], F32, two)
            junk = sb("junk", [128, NCB, KU], BF16, two)
            acc_d = sb("acc_d", [128, 2, GQ], F32, two)
            acc_p = sb("acc_p", [128, 2, GQ], F32, two)
            acc = sb("acc", [128, GQ], F32, two)
            diag = sb("diag", [128, GT, 128], F32, two)
            ident_r = sb("ident_r", [128, 128], F32R, two)
            ones = sb("ones", [128, D], F32, two)
            row_t = sb("row_t", [128, UR], F32, two)
            col_t = sb("col_t", [128, NCB, NCB, CB], F32, two)
            rrow_t = sb("rrow_t", [128, WR], F32, two)
            rcol_t = sb("rcol_t", [128, ND, CB], F32, two)
            rless_t = sb("rless_t", [128, ND, CB], F32, two)
            neg_lo_t = sb("neg_lo_t", [128, 1], F32, two)
            o_sum = sb("o_sum", [D, GQ], F32, two)
            o_out = sb("o_out", [D, GQ], F32, two)
            maxes = sb("maxes", [128, 2, GT, NCB], F32, two)
            neg_max = sb("neg_max", [128, 2, GT], F32R, two)
            inv_t = sb("inv_t", [128, GT], F32, two)
        n_rows = WR * CB
        sums_of = [rows_sum[:], *(pT.rearrange("p a h n -> p (a h n)")[:, k * n_rows:(k + 1) * n_rows]
                                  for k in range(2)), rows_sum[:]]
        with ExitStack() as three:
            o_in = sb("o_in", [128, 2, CT, TT], F32, three)
            x_in = sb("x_in", [128, 2, CT, TT], F32, three)
            y_out = sb("y_out", [128, 2, CT, TT], F32, three)
            o_hi = sb("o_hi", [128, 2, CT, TT], F32R, three)
            o_lo = sb("o_lo", [128, 2, CT, TT], F32R, three)
            wo_sb = sb("wo_sb", [128, CT, C], F32, three)
            wo_hi = sb("wo_hi", [128, CT, C], F32R, three)
            wo_lo = sb("wo_lo", [128, CT, C], F32R, three)

        ps = ctx.enter_context(nc.psum_tensor("ps", [128, 8, 512], F32))
        ps_slot = [ps[:, 2 * i:2 * i + 2, :] for i in range(NSLOT)]
        ps_o = ps[:, 6, :]
        ps_x = ps[:, 7, :]

        x_loaded = [sem(f"x_loaded{i}") for i in range(B * CT)]
        consts_loaded = sem("consts_loaded")
        w_loaded = sem("w_loaded")
        w_hi_done = sem("w_hi_done")
        w_lo_done = sem("w_lo_done")
        stats_own = sem("stats_own")
        stats_step = sem("stats_step")
        group_avg = sem("group_avg")
        root_done = sem("root_done")
        x_normed = sem("x_normed")
        x_hi_done = sem("x_hi_done")
        x_lo_done = sem("x_lo_done")
        proj_done = sem("proj_done")
        hi_done = sem("hi_done")
        lo_done = sem("lo_done")
        v_done = sem("v_done")
        qk_stored = [sem(f"qk_stored{i}") for i in range(4)]
        v_stored = [sem(f"v_stored{i}") for i in range(4)]

        ones_set = sem("ones_set")
        onehots_loaded = sem("onehots_loaded")
        onehots_set = sem("onehots_set")
        bias_in = sem("bias_in")
        rows_in = sem("rows_in")
        bias_ready = sem("bias_ready")
        cols_less = sem("cols_less")
        rows_summed = sem("rows_summed")
        rows_rounded = sem("rows_rounded")
        rows_ready = sem("rows_ready")
        k_mov_in = [sem(f"k_mov_in{c}") for c in range(NCB)]
        k_st_in = [sem(f"k_st_in{c}") for c in range(NCB)]
        k_rows_in = [sem(f"k_rows_in{k}") for k in range(2)]
        k_rows_set = sem("k_rows_set")
        q_hi_in = [sem(f"q_hi_in{k}") for k in range(3)]
        q_lo_in = [sem(f"q_lo_in{k}") for k in range(2)]
        v_in = [sem(f"v_in{c}") for c in range(NCB)]
        unit_filled = sem("unit_filled")
        unit_maxed = sem("unit_maxed")
        max_ready = sem("max_ready")
        max_row = sem("max_row")
        max_row_set = sem("max_row_set")
        pair_filled = sem("pair_filled")
        exp_done = sem("exp_done")
        pair_used = sem("pair_used")
        dve_added = sem("dve_added")
        pool_added = sem("pool_added")
        acc_merged = sem("acc_merged")
        acc_ready = sem("acc_ready")
        sums_ready = sem("sums_ready")
        inv_ready = sem("inv_ready")
        diag_ready = sem("diag_ready")
        bc_ready = sem("bc_ready")
        half_ready = sem("half_ready")
        o_summed = sem("o_summed")
        o_scaled = sem("o_scaled")
        o_stored = sem("o_stored")

        wo_loaded = sem("wo_loaded")
        o_loaded = [sem("o_loaded0"), sem("o_loaded1")]
        x_in_loaded = [sem("x_in_loaded0"), sem("x_in_loaded1")]
        wo_hi_done = sem("wo_hi_done")
        wo_lo_done = sem("wo_lo_done")
        o_hi_done = sem("o_hi_done")
        o_lo_done = sem("o_lo_done")
        out_proj = sem("out_proj")
        out_added = sem("out_added")
        out_stored = [sem("out_stored0"), sem("out_stored1")]

        PROJ0, LO0, V0, QKST0, VST0, OPROJ0, OADD0, OUT0 = 2 * NM, 8, 4, 32, 16, CT * B, CT * B, 16

        def wait(eng, s, value):
            if not (isinstance(value, int) and value <= 0):
                eng.wait_ge(s, value)

        def over_tiles(eng, tile, between=None):
            for b in range(B):
                def pair(i, ends):
                    for par in range(2):
                        t = 2 * i + par
                        tile(b * NTT + t, b, t, par,
                             (b, t + 1) if not (ends and par) else (b + 1, 0) if b + 1 < B else None)
                if b == 0:
                    tile(0, 0, 0, 0, (0, 1))
                    if between:
                        between()
                    tile(1, 0, 1, 1, (0, 2))
                with eng.Fori(1 if b == 0 else 0, NTT // 2 - 1) as i:
                    pair(i, False)
                pair(NTT // 2 - 1, True)

        def over_heads(eng, head):
            head(0, True, False)
            with eng.Fori(1, NIT - 1) as it:
                head(it, False, False)
            head(NIT - 1, False, True)

        def after(it, g):
            return (it, g + 1) if g + 1 < NG else (it + 1, 0)

        def before(it, g):
            return (it, g - 1) if g > 0 else (it - 1, NG - 1)

        def pair_free(eng, it, g, s):
            it, g, s = (it, g, s - PT) if s >= PT else (*before(it, g), s - PT + NP)
            G = it * NG + g
            if isinstance(G, int) and G < 0:
                return
            eng.wait_ge(pair_used, NP * G + s + 1)
            if s % 2 == 0:
                eng.wait_ge(dve_added, (NP // 2 - 1) * G + max(s // 2, 1))
            else:
                eng.wait_ge(pool_added, (NP // 2 - 1) * G + max(s // 2, 1))

        block = ctx.enter_context(nc.Block())

        @block.sync
        def _(sp):
            sp.dma_start(w_raw, w_qkv[0:128, :]).then_inc(w_loaded, 16)
            sp.dma_start(avg, avg_in).then_inc(consts_loaded, 16)
            sp.dma_start(ident[:], ident_in).then_inc(consts_loaded, 16)
            for b in range(B):
                for c in range(CT):
                    sp.dma_start(x_sb[:, b * CT + c, :], xT[b, c * 128:(c + 1) * 128, :]).then_inc(
                        x_loaded[b * CT + c], 16)
                    if b == 0 and c > 0:
                        sp.wait_ge(w_hi_done, c)
                        sp.wait_ge(w_lo_done, c)
                        sp.dma_start(w_raw, w_qkv[c * 128:(c + 1) * 128, :]).then_inc(w_loaded, 16)

            def store(n, b, t, par, following):
                for m in range(8):
                    sp.wait_ge(lo_done, LO0 + 8 * n + m + 1)
                    dram = q_dram if m < 4 else k_dram
                    for hh in range(2):
                        sp.dma_start(
                            dram[b * HEADS + 2 * (m % 4) + hh, :, :, bass.ds(t * TT, TT)].rearrange(
                                "l d n -> d l n"),
                            qk_stage[hh * D:(hh + 1) * D, m % 4].bitcast(F32),
                        ).then_inc(qk_stored[m % 4], 16)
                for s in range(4):
                    sp.wait_ge(v_done, V0 + 4 * n + s + 1)
                    sp.dma_start(
                        v_dram[b * HEADS:(b + 1) * HEADS, bass.ds(t * TT + s * 128, 128), :].rearrange(
                            "h t d -> t h d"),
                        v_stage[:, s, :].rearrange("p (h d) -> p h d", h=HEADS),
                    ).then_inc(v_stored[s], 16)

            over_tiles(sp, store)

            for s in range(4):
                sp.wait_ge(qk_stored[s], QKST0 + 32 * 2 * B * NTT)
                sp.wait_ge(v_stored[s], VST0 + 16 * B * NTT)
            sp.wait_ge(proj_done, PROJ0 + NM * B * NTT)

            def load_k(tensor, done, it, c):
                sp.dma_start(tensor[:, c * KU:(c + 1) * KU].bitcast(F32),
                             k_dram[it, :, :, c * KU:(c + 1) * KU].rearrange("l d n -> (l d) n")
                             ).then_inc(done[c], 16)

            def load_v(it, c):
                n = NA * 128
                sp.dma_start(v_sb[:, c * NA:(c + 1) * NA, :],
                             v_dram[it, c * n:(c + 1) * n, :].rearrange("(j p) d -> p j d", p=128)
                             ).then_inc(v_in[c], 16)

            def load_q_hi(it, g):
                for half in range(2):
                    sp.dma_start(q_hi[half * D:(half + 1) * D, g % 3].bitcast(F32),
                                 q_dram[it, 0, :, g * GQ:(g + 1) * GQ]).then_inc(q_hi_in[g % 3], 16)

            def load_q_lo(it, g):
                sp.dma_start(q_rows[0:D, g % 2].bitcast(F32),
                             q_dram[it, 1, :, g * GQ:(g + 1) * GQ]).then_inc(q_lo_in[g % 2], 16)

            def copy_k_hi(it, g):
                for qb in range(NQB):
                    sp.dma_start(k_rows[0:D, g % 2, qb].bitcast(F32), k_mov[0:D].bitcast(F32)
                                 ).then_inc(k_rows_in[g % 2], 16)

            def load_bias_tables(it):
                sp.dma_start(row_t[:], row_win[it]).then_inc(bias_in, 16)
                sp.dma_start(col_t[:], col_win[it]).then_inc(bias_in, 16)

            def load_row_tables(it):
                sp.dma_start(rrow_t[:], row_rows[it]).then_inc(rows_in, 16)
                sp.dma_start(rcol_t[:], col_rows[it]).then_inc(rows_in, 16)
                sp.dma_start(rless_t[:], col_less[it]).then_inc(rows_in, 16)

            for par in range(2):
                sp.dma_start(pT[D:128, 0, par, :], onehots).then_inc(onehots_loaded, 16)
            sp.dma_start(neg_lo_t[D:128], neg_lo).then_inc(onehots_loaded, 16)
            load_bias_tables(0)
            load_q_hi(0, 0)
            for c in range(NCB):
                load_k(k_mov, k_mov_in, 0, c)
            load_row_tables(0)
            load_q_lo(0, 0)
            load_q_hi(0, 1)
            for c in range(NCB):
                load_k(k_st, k_st_in, 0, c)
            for c in range(NCB):
                sp.wait_ge(k_mov_in[c], 16)
            copy_k_hi(0, 0)
            for c in range(NCB):
                load_v(0, c)

            def head(it, first, last):
                for g in range(NG):
                    G = it * NG + g
                    wait(sp, pair_filled, NP * G)
                    if g + 1 < NG or not last:
                        load_q_lo(*after(it, g))
                        if g + 1 == NG:
                            for c in range(NCB):
                                sp.wait_ge(k_mov_in[c], 16 * (it + 2))
                        copy_k_hi(*after(it, g))
                    if g + 2 < NG or not last:
                        load_q_hi(*after(*after(it, g)))
                    if g == 1 and not last:
                        sp.wait_ge(rows_summed, ND * (it + 1))
                        load_row_tables(it + 1)
                        sp.wait_ge(bias_ready, NCB * NCB * (it + 1))
                        load_bias_tables(it + 1)
                    if g == NG - 2 and not last:
                        sp.wait_ge(k_rows_in[1], 16 * NQB * NG // 2 * (it + 1))
                        for c in range(NCB):
                            sp.wait_ge(unit_filled, NU * (G + 2) - NCB + c + 1)
                            load_k(k_mov, k_mov_in, it + 1, c)
                    if not (first and g == 0):
                        sp.wait_ge(o_scaled, G)
                        pit, pg = before(it, g)
                        sp.dma_start(o_dram[pit, :, pg * GQ:(pg + 1) * GQ], o_out[:]).then_inc(o_stored, 16)
                    if g == NG - 1 and not last:
                        for c in range(NCB):
                            sp.wait_ge(pair_filled, NP * G + NP // NCB * (c + 1))
                            load_k(k_st, k_st_in, it + 1, c)
                            sp.wait_ge(pair_used, NP * G + NP // NCB * (c + 1))
                            load_v(it + 1, c)

            over_heads(sp, head)
            sp.wait_ge(o_scaled, NIT * NG)
            sp.dma_start(o_dram[NIT - 1, :, (NG - 1) * GQ:], o_out[:]).then_inc(o_stored, 16)

            def load_o(i, b):
                for c in range(CT):
                    sp.dma_start(o_in[:, b, c, :],
                                 o_dram[b * HEADS + 2 * c:b * HEADS + 2 * c + 2, :, bass.ds(i * TT, TT)]
                                 .rearrange("h d n -> (h d) n")).then_inc(o_loaded[b], 16)

            def load_x(i, b):
                sp.dma_start(x_in[:, b], xT[b, :, bass.ds(i * TT, TT)].rearrange("(c p) n -> p c n", p=128)
                             ).then_inc(x_in_loaded[b], 16)

            sp.dma_start(wo_sb[:], w_out.rearrange("(c p) n -> p c n", p=128)).then_inc(wo_loaded, 16)
            sp.wait_ge(o_stored, 16 * NIT * NG)
            for b in range(B):
                load_o(0, b)
            for b in range(B):
                load_x(0, b)

            def tile_out(i, last):
                if not last:
                    for b in range(B):
                        sp.wait_ge(o_lo_done, B * i + b + 1)
                        load_o(i + 1, b)
                for b in range(B):
                    sp.wait_ge(out_added, OADD0 + CT * (B * i + b + 1))
                    sp.dma_start(outT[b, :, bass.ds(i * TT, TT)].rearrange("(c p) n -> p c n", p=128),
                                 y_out[:, b]).then_inc(out_stored[b], 16)
                    if not last:
                        load_x(i + 1, b)

            with sp.Fori(0, NTT - 1) as i:
                tile_out(i, False)
            tile_out(NTT - 1, True)
            for b in range(B):
                sp.wait_ge(out_stored[b], OUT0 + 16 * NTT)

        @block.tensor
        def _(pe):
            pe.wait_ge(consts_loaded, 32)

            def averages(b):
                bank = NM * b % 8
                if b > 0:
                    pe.wait_ge(lo_done, LO0 + bank + 1)
                for k in range(2):
                    pe.wait_ge(stats_step, 3 * b + k + 1)
                    nc.tensor.matmul(ps[:, bank, 0:CT], avg, stat[:, k, b * CT:(b + 1) * CT],
                                     start=True, stop=True).then_inc(group_avg, 1)
                pe.wait_ge(stats_step, 3 * b + 3)

            averages(0)

            pe.wait_ge(w_hi_done, CT)
            pe.wait_ge(w_lo_done, CT)

            def project(n, b, t, par, following):
                pe.wait_ge(x_lo_done, n + 1)
                for m in range(NM):
                    was = m - 8 if m >= 8 else m + 4
                    of = n if m >= 8 else n - 1
                    if was < 8:
                        pe.wait_ge(lo_done, LO0 + 8 * of + was + 1)
                    else:
                        pe.wait_ge(v_done, V0 + 4 * of + was - 8 + 1)
                    bank = ps[:, (par * NM + m) % 8, :]
                    steps = [(w, x, c) for c in range(CT)
                             for w, x in ((w_hi, x_hi), (w_hi, x_lo), (w_lo, x_hi))]
                    for k, (w, x, c) in enumerate(steps):
                        if m < 8:
                            lhs, rhs = w[:, c, m * 128:(m + 1) * 128], x[:, par, c, :]
                        else:
                            lhs, rhs = x[:, par, c, (m - 8) * 128:(m - 7) * 128], w[:, c, 2 * C:3 * C]
                        mm = nc.tensor.matmul(bank, lhs, rhs, start=(k == 0), stop=(k == len(steps) - 1))
                    mm.then_inc(proj_done, 1)

            over_tiles(pe, project, lambda: averages(1))

            pe.wait_ge(lo_done, LO0 + 8 * B * NTT)
            pe.wait_ge(v_done, V0 + 4 * B * NTT)
            pe.wait_ge(ones_set, 1)

            def drained(it, g, fill, has_units):
                back, (kind, n) = user_before(FILLS.index(fill), lambda f: f[0] == "S" or has_units)
                G = it * NG + g - back
                if kind == "M":
                    wait(pe, unit_maxed, NU * (G + 1) + n + 1)
                else:
                    wait(pe, exp_done, NP * G + n + 1)

            def max_unit(it, g, u, slot):
                t, c = u // NCB, u % NCB
                if u == 0:
                    pe.wait_ge(q_hi_in[g % 3], 32 * (NG // 3 * it + g // 3 + 1))
                if g == 0 and t == 0:
                    pe.wait_ge(k_mov_in[c], 16 * (it + 1))
                for half in range(2):
                    mm = nc.tensor.matmul(
                        ps_slot[slot][:, half, :], q_hi[:, g % 3, t * 128:(t + 1) * 128],
                        k_mov[:, c * KU + half * 512:c * KU + (half + 1) * 512], start=True, stop=True)
                mm.then_inc(unit_filled, 1)

            def max_rows(it, g):
                pe.wait_ge(max_ready, GT * (it * NG + g + 1))
                for t in range(GT):
                    mm = nc.tensor.matmul(
                        ps_x[:, t * 128:(t + 1) * 128],
                        neg_max[:, g % 2, t:t + 1].to_broadcast([128, 128]), ident_r[:],
                        start=True, stop=True)
                mm.then_inc(max_row, 1)

            def score_pair(it, g, s, slot):
                G = it * NG + g
                if s == 0:
                    pe.wait_ge(q_lo_in[g % 2], 16 * (NG // 2 * it + g // 2 + 1))
                    pe.wait_ge(max_row_set, G + 1)
                    pe.wait_ge(k_rows_in[g % 2], 16 * NQB * (NG // 2 * it + g // 2 + 1))
                    pe.wait_ge(k_rows_set, NQB * NCB * (G + 1))
                if g == 0 and s % (NP // NCB) == 0:
                    pe.wait_ge(k_st_in[s // (NP // NCB)], 16 * (it + 1))
                for h in range(2):
                    j = 2 * s + h
                    bank = ps_slot[slot][:, h, :]
                    for qb in range(NQB):
                        n = GQ // NQB
                        nc.tensor.matmul(
                            bank[:, qb * n:(qb + 1) * n], k_rows[0:KB, g % 2, qb, j * 128:(j + 1) * 128],
                            q_rows[0:KB, g % 2, qb * n:(qb + 1) * n], start=(qb == 0), stop=False,
                            skip_group_check=True)
                    mm = nc.tensor.matmul(bank, k_st[:, j * 128:(j + 1) * 128], q_hi[:, g % 3, :],
                                          start=False, stop=True, skip_group_check=True)
                mm.then_inc(pair_filled, 1)

            def products(it, g, s):
                G = it * NG + g
                if s == 0:
                    wait(pe, o_summed, G)
                if g == 0 and s % (NP // NCB) == 0:
                    pe.wait_ge(v_in[s // (NP // NCB)], 16 * (it + 1))
                pe.wait_ge(exp_done, NP * G + s + 1)
                for h in range(2):
                    mm = nc.tensor.matmul(ps_o[h * D:(h + 1) * D, :], v_sb[:, 2 * s + h, :],
                                          pT[:, s % PT, h, :], start=(s == 0), stop=(s == NP - 1))
                mm.then_inc(pair_used, 1)

            def row_sums(it, g):
                pe.wait_ge(acc_ready, it * NG + g + 1)
                for t in range(GT):
                    mm = nc.tensor.matmul(ps_x[:, t:t + 1], acc[:, t * 128:(t + 1) * 128], ones[:, 0:1],
                                          start=True, stop=True)
                mm.then_inc(sums_ready, 1)

            def broadcast(it, g):
                pe.wait_ge(diag_ready, it * NG + g + 1)
                nc.tensor.matmul(ps_x[0:D, :], ones[:], diag.rearrange("p t n -> p (t n)"),
                                 start=True, stop=True).then_inc(bc_ready, 1)

            for u in range(NU):
                wait(pe, unit_maxed, u - NSLOT + 1)
                max_unit(0, 0, u, u % NSLOT)
            pe.wait_ge(onehots_set, 2)
            max_rows(0, 0)
            pe.wait_ge(unit_maxed, NU)

            def head(it, first, last):
                for g in range(NG):
                    has_units = not (last and g == NG - 1)
                    for s in range(NP):
                        if s == NP - 1 and has_units:
                            if not (first and g == 0):
                                pe.wait_ge(o_scaled, it * NG + g)
                            else:
                                pe.wait_ge(max_row_set, 1)
                            max_rows(*after(it, g))
                        for kind, n in FILLS:
                            if kind == "S" and n == s:
                                drained(it, g, (kind, n), has_units)
                                score_pair(it, g, n, FILLS.index((kind, n)) % NSLOT)
                            elif kind == "M" and UNIT_STEP[n] == s and has_units:
                                drained(it, g, (kind, n), has_units)
                                max_unit(*after(it, g), n, FILLS.index((kind, n)) % NSLOT)
                        if s > 0:
                            products(it, g, s - 1)
                        elif not (first and g == 0):
                            products(*before(it, g), NP - 1)
                        if not (first and g == 0):
                            if s == SUM_STEP:
                                row_sums(*before(it, g))
                            if s == BC_STEP:
                                broadcast(*before(it, g))

            over_heads(pe, head)
            products(NIT - 1, NG - 1, NP - 1)
            row_sums(NIT - 1, NG - 1)
            broadcast(NIT - 1, NG - 1)

            pe.wait_ge(wo_lo_done, 1)
            pe.wait_ge(o_scaled, NIT * NG)
            with pe.Fori(0, NTT) as i:
                for b in range(B):
                    pe.wait_ge(o_lo_done, B * i + b + 1)
                    pe.wait_ge(out_added, OADD0 + CT * (B * (i - 1) + b + 1))
                    for m in range(CT):
                        steps = [(w, o, c) for c in range(CT)
                                 for w, o in ((wo_hi, o_hi), (wo_hi, o_lo), (wo_lo, o_hi))]
                        for k, (w, o, c) in enumerate(steps):
                            mm = nc.tensor.matmul(ps[:, b * CT + m, :], w[:, c, m * 128:(m + 1) * 128],
                                                  o[:, b, c, :], start=(k == 0), stop=(k == len(steps) - 1))
                        mm.then_inc(out_proj, 1)

        @block.scalar
        def _(act):
            for c in range(CT):
                act.wait_ge(w_loaded, 16 * (c + 1))
                nc.scalar.activation(w_hi[:, c, :], w_raw, ACT.Copy).then_inc(w_hi_done, 1)
            def root(b):
                act.wait_ge(stats_step, 3 * b + 3)
                at = slice(b * CT, (b + 1) * CT)
                nc.scalar.activation(stat[:, 3, at], stat[:, 2, at], ACT.Sqrt).then_inc(root_done, 1)

            def split_x(n, b, t, par):
                act.wait_ge(x_normed, n + 1)
                nc.scalar.activation(x_hi[:, par], x_sb[:, b * CT:(b + 1) * CT, bass.ds(t * TT, TT)],
                                     ACT.Copy).then_inc(x_hi_done, 1)

            def evacuate(n, b, t, par, following):
                if following:
                    split_x(n + 1, *following, 1 - par)
                for m in range(NM):
                    act.wait_ge(proj_done, PROJ0 + NM * n + m + 1)
                    bank = ps[:, (par * NM + m) % 8, :]
                    if m < 8:
                        act.wait_ge(qk_stored[m % 4], QKST0 + 32 * (2 * n + m // 4))
                        nc.scalar.activation(qk_stage[:, m % 4, 0, :], bank, ACT.Copy,
                                             scale=SCALE if m < 4 else 1.0).then_inc(hi_done, 1)
                    else:
                        act.wait_ge(v_stored[m - 8], VST0 + 16 * n)
                        nc.scalar.activation(v_stage[:, m - 8, :], bank, ACT.Copy).then_inc(v_done, 1)

            root(0)
            split_x(0, 0, 0, 0)
            over_tiles(act, evacuate, lambda: root(1))

            act.wait_ge(proj_done, PROJ0 + NM * B * NTT)
            for s in range(4):
                act.wait_ge(qk_stored[s], QKST0 + 32 * 2 * B * NTT)
                act.wait_ge(v_stored[s], VST0 + 16 * B * NTT)
            act.wait_ge(onehots_loaded, 48)
            nc.scalar.activation(q_rows[D:128], pT[D:128, 0], ACT.Copy).then_inc(onehots_set, 1)
            act.wait_ge(consts_loaded, 32)
            nc.scalar.activation(ident_r[:], ident[:], ACT.Copy).then_inc(onehots_set, 1)

            def copy_rows(it, g, k):
                qb, c = k // NCB, k % NCB
                first_row = IMG_H - QB - QB * (NQB * (g % 2) + qb)
                nc.scalar.activation(
                    k_rows[D:128, g % 2, qb, c * KU:(c + 1) * KU],
                    rows[D:128, c - g // 2 + NCB - 1, first_row * CB:first_row * CB + KU].bitcast(F32),
                    ACT.Copy).then_inc(k_rows_set, 1)

            def set_max_row(it, g):
                act.wait_ge(max_row, it * NG + g + 1)
                nc.scalar.activation(q_rows[D:D + 1, g % 2, :], ps_x[0:1, :], ACT.Copy).then_inc(max_row_set, 1)

            def exp(it, g, s):
                G = it * NG + g
                pair_free(act, it, g, s)
                act.wait_ge(pair_filled, NP * G + s + 1)
                slot = FILLS.index(("S", s)) % NSLOT
                nc.scalar.activation(pT[:, s % PT], ps_slot[slot], ACT.Exp).then_inc(exp_done, 1)

            def half(it, g):
                act.wait_ge(pair_used, NP * (it * NG + g + 1))
                wait(act, o_scaled, it * NG + g)
                nc.scalar.activation(o_sum[:], ps_o[D:2 * D, :], ACT.Copy).then_inc(half_ready, 1)

            def round_rows(n, d):
                act.wait_ge(rows_summed, n + 1)
                sums = sums_of[n] if isinstance(n, int) and n < len(FIRST_ROWS) else rows_sum
                nc.scalar.activation(rows[D:128, d, :], sums[D:128], ACT.Copy).then_inc(rows_rounded, 1)

            for n in range(NCB):
                round_rows(n, FIRST_ROWS[n])
            for c in range(NCB):
                act.wait_ge(rows_ready, 2 * (c + 1))
                for qb in range(NQB):
                    copy_rows(0, 0, NCB * qb + c)
            round_rows(NCB, FIRST_ROWS[NCB])
            set_max_row(0, 0)

            def head(it, first, last):
                for g in range(NG):
                    for s in range(NP):
                        if s == HALF_STEP and not (first and g == 0):
                            half(*before(it, g))
                        if s == NP - 1 and not (last and g == NG - 1):
                            set_max_row(*after(it, g))
                        exp(it, g, s)
                        if s in TABLE_STEPS and not (last and g == NG - 1):
                            nit, ng = after(it, g)
                            if s == TABLE_STEPS[0] and ng % 2 == 0:
                                built = len(FIRST_ROWS) + ND * it + {0: 4, 2: 0, 4: 1}[ng]
                                act.wait_ge(rows_ready, 2 * built)
                            copy_rows(nit, ng, TABLE_STEPS.index(s))
                        for k, (bg, d, nxt) in enumerate(ROW_BUILDS):
                            if (bg, HI_STEP) == (g, s) and not (nxt and last):
                                act.wait_ge(k_rows_set, NQB * NCB * (it * NG + g + 2))
                                round_rows(len(FIRST_ROWS) + ND * it + k, d)

            over_heads(act, head)
            half(NIT - 1, NG - 1)

            act.wait_ge(wo_loaded, 16)
            nc.scalar.activation(wo_hi[:], wo_sb[:], ACT.Copy).then_inc(wo_hi_done, 1)
            with act.Fori(0, NTT) as i:
                for b in range(B):
                    act.wait_ge(o_loaded[b], 16 * CT * (i + 1))
                    act.wait_ge(out_proj, OPROJ0 + CT * (B * (i - 1) + b + 1))
                    nc.scalar.activation(o_hi[:, b], o_in[:, b], ACT.Copy).then_inc(o_hi_done, 1)

        @block.gpsimd
        def _(pool):
            pool.wait_ge(proj_done, PROJ0 + NM * B * NTT)
            for s in range(4):
                pool.wait_ge(qk_stored[s], QKST0 + 32 * 2 * B * NTT)
                pool.wait_ge(v_stored[s], VST0 + 16 * B * NTT)
            nc.gpsimd.memset(ones[:], 1.0).then_inc(ones_set, 1)
            group_reg = pool.alloc_register("groups")
            pool.reg_mov(group_reg, 0)

            def build_bias(it, cb, kb):
                pool.wait_ge(bias_in, 32 * (it + 1))
                nc.gpsimd.tensor_tensor(
                    bias[:, cb, kb, :].rearrange("p (u j) -> p u j", j=CB),
                    row_t[:].unsqueeze(2).to_broadcast([128, UR, CB]),
                    col_t[:, cb, kb, :].unsqueeze(1).to_broadcast([128, UR, CB]), ALU.add
                ).then_inc(bias_ready, 1)

            def sum_rows(n, d):
                early = isinstance(n, int) and n < len(FIRST_ROWS)
                if not early:
                    pool.wait_ge(rows_ready, 2 * n)
                elif n == NCB:
                    pool.wait_ge(rows_ready, 2)
                nc.gpsimd.tensor_tensor(
                    (sums_of[n] if early else rows_sum[:]).rearrange("p (u j) -> p u j", j=CB),
                    rrow_t[:].unsqueeze(2).to_broadcast([128, WR, CB]),
                    rcol_t[:, d, :].unsqueeze(1).to_broadcast([128, WR, CB]), ALU.add
                ).then_inc(rows_summed, 1)

            def subtract_columns(it):
                pool.wait_ge(rows_in, 48 * (it + 1))
                nc.gpsimd.tensor_tensor(rcol_t[:], rcol_t[:], rless_t[:], ALU.subtract
                                        ).then_inc(cols_less, 1)
                pool.wait_ge(cols_less, it + 1)

            def add_pair(it, g, s):
                G = it * NG + g
                n = (NP // 2 - 1) * G + s // 2
                if s == 3:
                    wait(pool, acc_merged, G)
                pool.wait_ge(exp_done, NP * G + s + 1)
                if s == 3:
                    src = pT[:, 1 % PT]
                else:
                    pool.wait_ge(pool_added, n - 1)
                    src = acc_p[:]
                nc.gpsimd.tensor_tensor(acc_p[:], src, pT[:, s % PT], ALU.add).then_inc(pool_added, 1)

            def diagonals(it, g):
                pool.reg_add(group_reg, group_reg, 1)
                pool.wait_ge(consts_loaded, 32)
                pool.wait_ge(inv_ready, group_reg)
                for t in range(GT):
                    op = nc.gpsimd.tensor_scalar(diag[:, t, :], ident[:], inv_t[:, t:t + 1], None, ALU.mult)
                op.then_inc(diag_ready, 1)

            for kb in range(NCB):
                build_bias(0, 0, kb)
            subtract_columns(0)
            pool.wait_ge(onehots_set, 1)
            for n, d in enumerate(FIRST_ROWS):
                sum_rows(n, d)
            for kb in range(NCB):
                build_bias(0, 1, kb)

            def head(it, first, last):
                for g in range(NG):
                    G = it * NG + g
                    for s in range(NP):
                        if s == 0 and not (first and g == 0):
                            add_pair(*before(it, g), NP - 1)
                        if s >= 4 and s % 2 == 0:
                            add_pair(it, g, s - 1)
                        if s == DIAG_STEP and not (first and g == 0):
                            diagonals(*before(it, g))
                        what = BUILDS.get((g, s))
                        if what is None or (what[-1] and last):
                            continue
                        if what[0] == "E":
                            wait(pool, unit_maxed, NU * (G + 1))
                            build_bias(it + what[-1], what[1], what[2])
                        else:
                            k = ROW_BUILDS.index((g, *what[1:]))
                            if k == 1:
                                subtract_columns(it + 1)
                            sum_rows(len(FIRST_ROWS) + ND * it + k, what[1])

            over_heads(pool, head)
            add_pair(NIT - 1, NG - 1, NP - 1)
            diagonals(NIT - 1, NG - 1)

        @block.vector
        def _(dve):
            unit_reg = dve.alloc_register("units")
            dve.reg_mov(unit_reg, 0)
            for s, value in ((proj_done, PROJ0), (lo_done, LO0), (v_done, V0),
                             (out_proj, OPROJ0), (out_added, OADD0),
                             *((q, QKST0) for q in qk_stored), *((q, VST0) for q in v_stored),
                             *((q, OUT0) for q in out_stored)):
                dve.sem_inc(s, value)

            own_n = 0

            def own(op):
                nonlocal own_n
                own_n += 1
                op.then_inc(stats_own, 1)
                dve.wait_ge(stats_own, own_n)

            V = nc.vector

            def channel_stats(b):
                for i in range(b * CT, (b + 1) * CT):
                    if i < CT:
                        dve.wait_ge(w_hi_done, i + 1)
                        V.tensor_tensor(w_lo[:, i, :], w_raw, w_hi[:, i, :].bitcast(F32), ALU.subtract
                                        ).then_inc(w_lo_done, 1)
                    dve.wait_ge(x_loaded[i], 16)
                    for k in range(NTT):
                        op = V.bn_stats(bn[:, k, :], x_sb[:, i, k * TT:(k + 1) * TT])
                    own(op)
                    own(V.bn_aggr(mv[:, i, :], bn))
                at = slice(b * CT, (b + 1) * CT)
                V.tensor_copy(stat[:, 0, at], mv[:, at, 0]).then_inc(stats_step, 1)

            def group_stats(b):
                at = slice(b * CT, (b + 1) * CT)
                bank = NM * b % 8
                dve.wait_ge(group_avg, 2 * b + 1)
                own(V.tensor_copy(stat[:, 4, at], ps[:, bank, 0:CT]))
                own(V.tensor_tensor(stat[:, 5, at], stat[:, 0, at], stat[:, 4, at], ALU.subtract))
                own(V.tensor_tensor(stat[:, 6, at], stat[:, 5, at], stat[:, 5, at], ALU.mult))
                V.tensor_tensor(stat[:, 1, at], stat[:, 6, at], mv[:, at, 1], ALU.add).then_inc(stats_step, 1)
                dve.wait_ge(group_avg, 2 * b + 2)
                V.tensor_scalar(stat[:, 2, at], ps[:, bank, 0:CT], EPS, None, ALU.add).then_inc(stats_step, 1)
                dve.wait_ge(root_done, b + 1)
                own(V.reciprocal(stat[:, 5, at], stat[:, 3, at]))
                own(V.tensor_tensor(stat[:, 6, at], stat[:, 2, at], stat[:, 5, at], ALU.mult))
                own(V.tensor_tensor(stat[:, 7, at], stat[:, 6, at], stat[:, 3, at], ALU.add))
                own(V.tensor_scalar(stat[:, 5, at], stat[:, 7, at], 0.5, None, ALU.mult))
                own(V.reciprocal(stat[:, 8, at], stat[:, 5, at]))

            def prepare(n, b, t, par):
                dve.wait_ge(proj_done, PROJ0 + NM * (n - 1))
                for c in range(CT):
                    k = b * CT + c
                    x = x_sb[:, k, bass.ds(t * TT, TT)]
                    op = V.tensor_scalar(x, x, stat[:, 4, k:k + 1], stat[:, 8, k:k + 1],
                                         ALU.subtract, ALU.mult)
                op.then_inc(x_normed, 1)
                dve.wait_ge(x_hi_done, n + 1)
                V.tensor_tensor(x_lo[:, par], x_sb[:, b * CT:(b + 1) * CT, bass.ds(t * TT, TT)],
                                x_hi[:, par].bitcast(F32), ALU.subtract).then_inc(x_lo_done, 1)

            def low_qk(n, b, t, par, following):
                if following:
                    prepare(n + 1, *following, 1 - par)
                if isinstance(n, int) and n == 0:
                    channel_stats(1)
                for m in range(8):
                    dve.wait_ge(hi_done, 8 * n + m + 1)
                    stage = qk_stage[:, m % 4]
                    V.scalar_tensor_tensor(
                        out=stage[:, 1, :], in0=ps[:, (par * NM + m) % 8, :],
                        scalar=SCALE if m < 4 else 1.0, in1=stage[:, 0, :].bitcast(F32),
                        op0=ALU.mult, op1=ALU.subtract).then_inc(lo_done, 1)

            channel_stats(0)
            group_stats(0)
            prepare(0, 0, 0, 0)
            over_tiles(dve, low_qk, lambda: group_stats(1))

            dve.wait_ge(proj_done, PROJ0 + NM * B * NTT)
            for s in range(4):
                dve.wait_ge(qk_stored[s], QKST0 + 32 * 2 * B * NTT)
                dve.wait_ge(v_stored[s], VST0 + 16 * B * NTT)
            dve.wait_ge(onehots_loaded, 48)

            def low_rows(n, d, part):
                dve.wait_ge(rows_rounded, n + 1)
                at = slice(part * WR // 2 * CB, (part + 1) * WR // 2 * CB)
                r = rows[D:128, d, at]
                sums = sums_of[n] if isinstance(n, int) and n < len(FIRST_ROWS) else rows_sum
                nc.vector.scalar_tensor_tensor(
                    out=r, in0=r.bitcast(F32), scalar=neg_lo_t[D:128], in1=sums[D:128, at],
                    op0=ALU.mult, op1=ALU.add).then_inc(rows_ready, 1)

            def max_unit(it, g, u):
                G, t, c = it * NG + g, u // NCB, u % NCB
                U = NU * G + u
                tile = g * GT + t
                cb, a = tile // NA, tile % NA
                if isinstance(G, int) and G == 0 and t == 0:
                    dve.wait_ge(bias_ready, c + 1)
                elif g % 2 == 0 and u == 0:
                    dve.wait_ge(bias_ready, NCB * (NCB * it + cb + 1))
                dve.reg_add(unit_reg, unit_reg, 1)
                dve.wait_ge(stats_step, 3)
                dve.wait_ge(unit_filled, unit_reg)
                row = (IMG_H - TR - TR * a) * CB
                slot = u % NSLOT if isinstance(U, int) and U < NU else FILLS.index(("M", u)) % NSLOT
                nc.vector.tensor_tensor_reduce(
                    out=junk[:, c, :], in0=ps_slot[slot].rearrange("p a n -> p (a n)"),
                    in1=bias[:, cb, c, row:row + KU], scale=1.0, scalar=LOWEST,
                    op0=ALU.add, op1=ALU.max, accum_out=maxes[:, g % 2, t, c:c + 1]).then_inc(unit_maxed, 1)
                if c == NCB - 1:
                    dve.wait_ge(unit_maxed, U + 1)
                    nc.vector.tensor_reduce(neg_max[:, g % 2, t:t + 1], maxes[:, g % 2, t, :], AX_X, ALU.max,
                                            negate=True).then_inc(max_ready, 1)

            def add_pair(it, g, s):
                G = it * NG + g
                n = (NP // 2 - 1) * G + s // 2
                dve.wait_ge(exp_done, NP * G + s + 1)
                if s == 2:
                    wait(dve, acc_ready, G)
                    src = pT[:, 0]
                else:
                    dve.wait_ge(dve_added, n - 1)
                    src = acc_d[:]
                nc.vector.tensor_tensor(acc_d[:], src, pT[:, s % PT], ALU.add).then_inc(dve_added, 1)

            def merge(it, g):
                G = it * NG + g
                dve.wait_ge(pool_added, (NP // 2 - 1) * (G + 1))
                dve.wait_ge(dve_added, (NP // 2 - 1) * (G + 1))
                nc.vector.tensor_tensor(acc_d[:], acc_d[:], acc_p[:], ALU.add).then_inc(acc_merged, 1)
                dve.wait_ge(acc_merged, G + 1)
                nc.vector.tensor_tensor(acc[:], acc_d[:, 0, :], acc_d[:, 1, :], ALU.add).then_inc(acc_ready, 1)

            def inverse(it, g):
                dve.wait_ge(sums_ready, it * NG + g + 1)
                nc.vector.reciprocal(inv_t[:], ps_x[:, 0:GT]).then_inc(inv_ready, 1)

            def add_half(it, g):
                G = it * NG + g
                dve.wait_ge(half_ready, G + 1)
                nc.vector.tensor_tensor(o_sum[:], ps_o[0:D, :], o_sum[:], ALU.add).then_inc(o_summed, 1)

            def output(it, g):
                G = it * NG + g
                dve.wait_ge(bc_ready, G + 1)
                wait(dve, o_stored, 16 * G)
                dve.wait_ge(o_summed, G + 1)
                nc.vector.tensor_tensor(o_out[:], ps_x[0:D, :], o_sum[:], ALU.mult).then_inc(o_scaled, 1)

            for u in range(NU):
                max_unit(0, 0, u)
                n = u // NCB - 1
                if u % NCB == NCB - 1 and n >= 0:
                    low_rows(n, FIRST_ROWS[n], 0)
                    low_rows(n, FIRST_ROWS[n], 1)
            low_rows(NCB, FIRST_ROWS[NCB], 0)
            low_rows(NCB, FIRST_ROWS[NCB], 1)

            def head(it, first, last):
                for g in range(NG):
                    for s in range(NP):
                        if not (first and g == 0):
                            if s == ADD_STEP:
                                add_half(*before(it, g))
                            if s == MERGE_STEP:
                                merge(*before(it, g))
                            if s == INV_STEP:
                                inverse(*before(it, g))
                            if s == OUT_STEP:
                                output(*before(it, g))
                        if s >= 3 and s % 2 == 1:
                            add_pair(it, g, s - 1)
                        if not (last and g == NG - 1):
                            for u in range(NU):
                                if UNIT_STEP[u] == s:
                                    max_unit(*after(it, g), u)
                        for k, (bg, d, nxt) in enumerate(ROW_BUILDS):
                            if bg == g and s in LO_STEPS and not (nxt and last):
                                low_rows(len(FIRST_ROWS) + ND * it + k, d, LO_STEPS.index(s))

            over_heads(dve, head)
            add_half(NIT - 1, NG - 1)
            merge(NIT - 1, NG - 1)
            inverse(NIT - 1, NG - 1)
            output(NIT - 1, NG - 1)

            dve.wait_ge(wo_hi_done, 1)
            nc.vector.tensor_tensor(wo_lo[:], wo_sb[:], wo_hi[:].bitcast(F32), ALU.subtract
                                    ).then_inc(wo_lo_done, 1)

            def low_o(i, b):
                dve.wait_ge(o_hi_done, B * i + b + 1)
                nc.vector.tensor_tensor(o_lo[:, b], o_in[:, b], o_hi[:, b].bitcast(F32), ALU.subtract
                                        ).then_inc(o_lo_done, 1)

            def add_x(i, b):
                dve.wait_ge(out_stored[b], OUT0 + 16 * i)
                dve.wait_ge(x_in_loaded[b], 16 * (i + 1))
                for m in range(CT):
                    dve.wait_ge(out_proj, OPROJ0 + CT * (B * i + b) + m + 1)
                    nc.vector.tensor_tensor(y_out[:, b, m, :], ps[:, b * CT + m, :], x_in[:, b, m, :],
                                            ALU.add).then_inc(out_added, 1)

            low_o(0, 0)
            with dve.Fori(0, NTT - 1) as i:
                low_o(i, 1)
                add_x(i, 0)
                low_o(i + 1, 0)
                add_x(i, 1)
            low_o(NTT - 1, 1)
            add_x(NTT - 1, 0)
            add_x(NTT - 1, 1)


def kernel(x, L0_conv_w_qkv, L0_conv_w_out, L0_conv_rel_row_tab, L0_conv_rel_col_tab):
    from concourse import bacc
    from concourse.bass_utils import run_bass_kernel_spmd

    row_tab, col_tab = np.asarray(L0_conv_rel_row_tab), np.asarray(L0_conv_rel_col_tab)
    xT = np.asarray(x).reshape(B, IMG_H, NCB, CB, C).transpose(0, 4, 2, 1, 3).reshape(B, C, S)
    p = np.arange(128)
    row_at = (p // CB)[:, None] - np.arange(UR)[None, :] + (IMG_H - TR) + IMG_H - 1
    blocks = np.arange(NCB) * CB
    col = np.arange(CB)
    col_at = ((p % CB)[:, None, None, None] + blocks[None, :, None, None] - blocks[None, None, :, None]
              - col[None, None, None, :] + IMG_W - 1)
    r_at = np.arange(QB)[:, None] - np.arange(WR)[None, :] + (IMG_H - QB) + IMG_H - 1
    c_at = (col[:, None, None] - (np.arange(ND) - (NCB - 1))[None, :, None] * CB - col[None, None, :]
            + IMG_W - 1)
    R, Cc = row_tab.T[:, r_at], col_tab.T[:, c_at]
    row_rows = np.zeros((HEADS, 128, WR), row_tab.dtype)
    col_rows = np.zeros((HEADS, 128, ND, CB), col_tab.dtype)
    col_less = np.zeros((HEADS, 128, ND, CB), col_tab.dtype)
    neg_lo = np.zeros((64, 1), np.float32)
    hots = np.zeros((64, GQ), np.float32)
    col_rows[:, D] = 1
    q = np.arange(GQ)
    q_row, q_col = q // CB % QB, q % CB
    for part in range(2):
        r0, c0 = 1 + part * QB, 1 + 2 * QB + part * (CB - 1)
        row_rows[:, D + r0:D + r0 + QB] = R
        col_rows[:, D + r0:D + r0 + QB] = Cc[:, 0:1]
        col_rows[:, D + c0:D + c0 + CB - 1] = Cc[:, 1:]
        col_less[:, D + c0:D + c0 + CB - 1] = Cc[:, 0:1]
        hots[r0:r0 + QB] = q_row == np.arange(QB)[:, None]
        hots[c0:c0 + CB - 1] = q_col == np.arange(1, CB)[:, None]
        if part == 1:
            neg_lo[r0:r0 + QB] = -1
            neg_lo[c0:c0 + CB - 1] = -1
    group = np.arange(128) // NORM_G
    arrays = {
        "xT": xT, "w_qkv": np.asarray(L0_conv_w_qkv), "w_out": np.asarray(L0_conv_w_out),
        "row_win": np.tile(row_tab.T[:, row_at], (B, 1, 1)),
        "col_win": np.tile(col_tab.T[:, col_at], (B, 1, 1, 1, 1)),
        "row_rows": np.tile(row_rows, (B, 1, 1)), "col_rows": np.tile(col_rows, (B, 1, 1, 1)),
        "col_less": np.tile(col_less, (B, 1, 1, 1)), "neg_lo": neg_lo, "onehots": hots,
        "ident": np.eye(128, dtype=np.float32),
        "avg": ((group[:, None] == group[None, :]) / NORM_G).astype(np.float32),
    }
    arrays = {f"in_{k}": np.ascontiguousarray(v) for k, v in arrays.items()}
    nc = bacc.Bacc("TRN2", target_bir_lowering=False, num_devices=1)
    aps = [nc.dram_tensor(k, v.shape, mybir.dt.from_np(v.dtype), kind="ExternalInput").ap()
           for k, v in arrays.items()]
    out = nc.dram_tensor("outT", (B, C, S), F32, kind="ExternalOutput").ap()
    attention_kernel(nc, *aps, out)
    result = run_bass_kernel_spmd(nc, [arrays], core_ids=[0]).results[0]["outT"]
    return np.ascontiguousarray(
        result.reshape(B, C, NCB, IMG_H, CB).transpose(0, 3, 2, 4, 1).reshape(B, IMG_H, IMG_W, C))
```
